# Optimizing a Trainium2 kernel written in Bass

```python
import numpy as np
import jax
import jax.numpy as jnp

def _softmax(x, axis=-1):
    return jax.nn.softmax(x, axis=axis)

def _gelu(x):
    return jax.nn.gelu(x, approximate=True)

def _silu(x):
    return jax.nn.silu(x)

def _sigmoid(x):
    return jax.nn.sigmoid(x)

def _layernorm(x, axis=-1, eps=1e-05):
    m = jnp.mean(x, axis=axis, keepdims=True)
    v = jnp.var(x, axis=axis, keepdims=True)
    return (x - m) / jnp.sqrt(v + eps)

def _scatter_add(tgt, idx, src, axis=0):
    return tgt.at[idx].add(src)

def _segment_sum(src, seg, n):
    return jax.ops.segment_sum(src, seg, n)
kernel_name = 'mk_gnn_resnorm_d2_gnn_r8_f06fcd'

def setup_inputs(seed: int=0):
    np.random.seed(seed)
    _w = jnp.asarray

    def _rec_inputs():
        import jax
        import jax.numpy as jnp
        _gk = jax.random.key(seed)
        x = -0.0003713 + 1 * jax.random.normal(jax.random.fold_in(_gk, 1), (12500, 128), jnp.float32)
        _s = jax.random.randint(jax.random.fold_in(_gk, 2), (100000,), 0, 12500, jnp.int32)
        _d = jax.random.randint(jax.random.fold_in(_gk, 3), (100000,), 0, 12500, jnp.int32)
        _loop = jnp.arange(12500, dtype=jnp.int32)
        src = jnp.concatenate([_s, _d, _loop])
        dst = jnp.concatenate([_d, _s, _loop])
        _o = jnp.argsort(dst, stable=True)
        src = src[_o]
        dst = dst[_o]
        edge_attr_128 = -8.16379e-05 + 0.999858 * jax.random.normal(jax.random.fold_in(_gk, 12), (212500, 128), jnp.float32)
        edge_weight = jax.random.uniform(jax.random.fold_in(_gk, 13), (212500,), jnp.float32, 0.0, 1)
        return (x, src, dst, edge_attr_128, edge_weight)
    x, src, dst, edge_attr_128, edge_weight = _rec_inputs()

    def _L0_gnn_setup():
        import jax, jax.numpy as jnp
        import numpy as np
        N_NODES = 12500
        key = jax.random.key(seed)
        k1, k2, k3, k4, k5 = jax.random.split(key, 5)
        E = 400000
        F_IN, F_OUT = (128, 128)
        x = jax.random.normal(k1, (N_NODES, F_IN), dtype=jnp.float32)
        row = jax.random.randint(k2, (E,), 0, N_NODES, dtype=jnp.int32)
        col = jax.random.randint(k3, (E,), 0, N_NODES, dtype=jnp.int32)
        edge_vals = jax.random.uniform(k4, (E,), dtype=jnp.float32)
        limit = float(np.sqrt(6.0 / (F_IN + F_OUT)))
        W = jax.random.uniform(k5, (F_IN, F_OUT), dtype=jnp.float32, minval=-limit, maxval=limit)
        b = jnp.zeros((F_OUT,), dtype=jnp.float32)
        return {'x': x, 'row': row, 'col': col, 'edge_vals': edge_vals, 'W': W, 'b': b}
    _L0_gnn_all = _L0_gnn_setup()
    _L0_gnn_in = {k: v for k, v in _L0_gnn_all.items() if k in ('W', 'b')}
    del _L0_gnn_all

    def _L1_gnn_setup():
        import jax, jax.numpy as jnp
        import numpy as np
        LN_EPS = 1e-05
        N, E, D = (6250, 100000, 128)
        H = 4 * D
        key = jax.random.key(seed)
        ks = jax.random.split(key, 8)
        h = jax.random.normal(ks[0], (N, D), dtype=jnp.float32)
        e_ij = jax.random.normal(ks[1], (E, D), dtype=jnp.float32)
        src = jax.random.randint(ks[2], (E,), 0, N, dtype=jnp.int32)
        dst = jax.random.randint(ks[3], (E,), 0, N, dtype=jnp.int32)
        W1 = jax.random.normal(ks[4], (D, H), dtype=jnp.float32) / np.sqrt(D)
        b1 = jnp.zeros((H,), dtype=jnp.float32)
        W2 = jax.random.normal(ks[5], (H, D), dtype=jnp.float32) / np.sqrt(H)
        b2 = jnp.zeros((D,), dtype=jnp.float32)
        gamma = jnp.ones((D,), dtype=jnp.float32)
        beta = jnp.zeros((D,), dtype=jnp.float32)
        return {'h': h, 'e_ij': e_ij, 'src': src, 'dst': dst, 'W1': W1, 'b1': b1, 'W2': W2, 'b2': b2, 'gamma': gamma, 'beta': beta}
    _L1_gnn_all = _L1_gnn_setup()
    _L1_gnn_in = {k: v for k, v in _L1_gnn_all.items() if k in ('W1', 'b1', 'W2', 'b2', 'gamma', 'beta')}
    del _L1_gnn_all
    return {'x': x, 'src': src, 'dst': dst, 'edge_attr_128': edge_attr_128, 'edge_weight': edge_weight, 'L0_gnn_W': _L0_gnn_in['W'], 'L0_gnn_b': _L0_gnn_in['b'], 'L1_gnn_W1': _L1_gnn_in['W1'], 'L1_gnn_b1': _L1_gnn_in['b1'], 'L1_gnn_W2': _L1_gnn_in['W2'], 'L1_gnn_b2': _L1_gnn_in['b2'], 'L1_gnn_gamma': _L1_gnn_in['gamma'], 'L1_gnn_beta': _L1_gnn_in['beta']}

def reference(x, src, dst, edge_attr_128, edge_weight, L0_gnn_W, L0_gnn_b, L1_gnn_W1, L1_gnn_b1, L1_gnn_W2, L1_gnn_b2, L1_gnn_gamma, L1_gnn_beta):
    import jax
    import jax.numpy as jnp

    def _L0_gnn_ref(x, row, col, edge_vals, W, b):
        import jax, jax.numpy as jnp
        import numpy as np
        N_NODES = 12500
        gathered = edge_vals[:, None] * x[col]
        ax = jax.ops.segment_sum(gathered, row, num_segments=N_NODES)
        return ax @ W + b

    def _L1_gnn_ref(h, e_ij, src, dst, W1, b1, W2, b2, gamma, beta):
        import jax, jax.numpy as jnp
        import numpy as np
        LN_EPS = 1e-05
        N = h.shape[0]
        neigh = jax.ops.segment_sum(h[src], dst, num_segments=N)
        u_edge = jax.ops.segment_sum(e_ij, dst, num_segments=N)
        u = neigh + u_edge
        hid = jax.nn.relu(u @ W1 + b1)
        out = hid @ W2 + b2 + h
        mean = jnp.mean(out, axis=-1, keepdims=True)
        var = jnp.var(out, axis=-1, keepdims=True)
        normed = (out - mean) * jax.lax.rsqrt(var + LN_EPS)
        return normed * gamma + beta
    x = _layernorm(x + _L0_gnn_ref(x, src, dst, edge_weight, L0_gnn_W, L0_gnn_b), axis=-1)
    x = _layernorm(x + _L1_gnn_ref(x, edge_attr_128, src, dst, L1_gnn_W1, L1_gnn_b1, L1_gnn_W2, L1_gnn_b2, L1_gnn_gamma, L1_gnn_beta), axis=-1)
    return x

_drawn_inputs = setup_inputs


def setup_inputs(seed=0):
    import zlib

    import numpy as np

    out = dict(_drawn_inputs(seed))
    spreads = {'L0_gnn_b': (0.0, 0.1),
     'L1_gnn_b1': (0.0, 0.767),
     'L1_gnn_b2': (0.0, 0.537),
     'L1_gnn_gamma': (1.0, 0.2),
     'L1_gnn_beta': (0.0, 0.1)}
    factors = {}
    for name, (base, spread) in spreads.items():
        noise = np.random.default_rng([zlib.crc32(name.encode()), seed]).standard_normal(out[name].shape)
        drawn = base * np.exp(spread * noise) if base else spread * noise
        out[name] = jnp.asarray(drawn.astype(out[name].dtype))
    for name, factor in factors.items():
        out[name] = (out[name] * factor).astype(out[name].dtype)
    return out
```

```python
import concourse.bass as bass
from concourse import mybir
from contextlib import ExitStack

F32 = mybir.dt.float32
I32 = mybir.dt.int32
ALU = mybir.AluOpType
ACT = mybir.ActivationFunctionType
AX = mybir.AxisListType

P = 128
COLS = 8
GROUP = COLS * P
HALF = 4
WIN = 128
TABLES = 4
EPS = 1e-5


class Shapes:

    def __init__(self, x, edge_attr, w1):
        self.nodes, self.feat = x.shape
        self.edges = edge_attr.shape[0]
        self.hidden = w1.shape[1]
        assert self.feat == P and self.hidden % P == 0
        self.groups = 2 * -(-self.edges // (2 * GROUP))
        self.cols = self.groups * COLS
        self.pads = self.groups * GROUP - self.edges
        self.tail = self.edges - (self.groups - 1) * GROUP
        assert 0 < self.tail < GROUP
        self.rows = P * (-(-self.nodes // P) + 1)
        self.chunk = HALF * P
        self.chunks = -(-self.nodes // self.chunk)


def allocator(nc, ctx):
    sb = lambda name, shape, dt=F32: ctx.enter_context(nc.sbuf_tensor(name, shape, dt))
    ps = lambda name, shape: ctx.enter_context(nc.psum_tensor(name, shape, F32))
    sem = lambda name: ctx.enter_context(nc.semaphore(name))
    return sb, ps, sem


class Kept:

    def __init__(self, nc, ctx, s):
        sb, _, self_sem = allocator(nc, ctx)
        self.ident = sb("ident", [P, P])
        self.ones = sb("ones", [P, P])
        self.earlier = sb("earlier", [P, P])
        self.iota = sb("iota", [P, P])
        self.spare = sb("spare", [P, 1])
        self.src_f = sb("src_f", [P, s.cols + HALF])
        self.dst_f = sb("dst_f", [P, s.cols])
        self.rel = sb("rel", [P, s.cols])
        self.weight = sb("weight", [P, s.cols])
        self.base = sb("base", [1, s.groups], I32)
        self.outside = sb("outside", [1, 1], I32)
        self.w = sb("w_sb", [P, P])
        self.b = sb("b_sb", [1, P])
        self.w1 = sb("w1_sb", [P, s.hidden])
        self.b1 = sb("b1_sb", [P, s.hidden // P])
        self.w2 = sb("w2_sb", [P, s.hidden // P, P])
        self.b2 = sb("b2_sb", [1, P])
        self.gamma = sb("gamma_sb", [1, P])
        self.beta = sb("beta_sb", [1, P])
        self.gamma_all = sb("gamma_all", [P, P])
        self.beta_all = sb("beta_all", [P, P])
        self.eps = sb("eps_sb", [P, 1])
        self.turn = self_sem("turn")


def passed(engine, kept):
    engine.sem_inc(kept.turn)


def prepare(nc, s, kept, src, dst, weight, w, b, w1, b1, w2, b2, gamma, beta, tables):
    with ExitStack() as ctx:
        sb, ps, sem = allocator(nc, ctx)
        src_i = sb("src_i", [P, s.cols], I32)
        dst_i = sb("dst_i", [P, s.cols], I32)
        base_f = sb("base_f", [1, s.groups])
        under = sb("under", [P, s.cols])
        over = sb("over", [P, s.cols])
        count = sb("count", [P, 1])
        zeros = sb("zeros", [P, s.rows])
        ps_base = ps("ps_base", [P, 512])
        ps_count = ps("ps_count", [P, 512])
        ps_gamma = ps("ps_gamma", [P, 512])
        consts_set = sem("consts_set")
        masks_ready = sem("masks_ready")
        indices_loaded = sem("indices_loaded")
        weights_loaded = sem("weights_loaded")
        zeros_set = sem("zeros_set")
        tables_zeroed = sem("tables_zeroed")
        floats_ready = sem("floats_ready")
        base_ready = sem("base_ready")
        base_spread = sem("base_spread")
        rel_ready = sem("rel_ready")
        marks_ready = sem("marks_ready")
        marks_joined = sem("marks_joined")
        count_ready = sem("count_ready")
        total_ready = sem("total_ready")
        gamma_spread = sem("gamma_spread")
        finished = sem("finished")
        block = ctx.enter_context(nc.Block())

        @block.sync
        def _(sp):
            sp.dma_start(src_i[:], src).then_inc(indices_loaded, 16)
            sp.dma_start(dst_i[:], dst).then_inc(indices_loaded, 16)
            sp.dma_start(kept.weight[:], weight).then_inc(weights_loaded, 16)
            sp.dma_start(kept.w[:], w).then_inc(weights_loaded, 16)
            sp.dma_start(kept.w1[:], w1).then_inc(weights_loaded, 16)
            sp.dma_start(kept.w2[:], w2.rearrange("(j p) f -> p j f", p=P)).then_inc(weights_loaded, 16)
            sp.dma_start(kept.b1[:], b1).then_inc(weights_loaded, 16)
            for row, vector in ((kept.b, b), (kept.b2, b2), (kept.gamma, gamma), (kept.beta, beta)):
                sp.dma_start(row[:], vector).then_inc(weights_loaded, 16)
            sp.wait_ge(weights_loaded, 16 * 9)

        @block.scalar
        def _(act):
            act.wait_ge(zeros_set, 1)
            for table in tables:
                act.dma_start(table.rearrange("(p c) f -> p (c f)", p=P), zeros[:]).then_inc(tables_zeroed, 16)
            act.wait_ge(tables_zeroed, 16 * len(tables))

        @block.gpsimd
        def _(pool):
            pool.memset(kept.ident[:], 0.0).then_inc(consts_set, 1)
            pool.memset(kept.ones[:], 1.0).then_inc(consts_set, 1)
            pool.memset(kept.eps[:], EPS).then_inc(consts_set, 1)
            pool.wait_ge(consts_set, 3)
            pool.affine_select(out=kept.ident[:], in_=kept.ident[:], compare_op=ALU.not_equal, fill=1.0,
                               base=0, pattern=[[-1, P]], channel_multiplier=1).then_inc(masks_ready, 1)
            pool.affine_select(out=kept.earlier[:], in_=kept.ones[:], compare_op=ALU.is_gt, fill=0.0,
                               base=0, pattern=[[-1, P]], channel_multiplier=1).then_inc(masks_ready, 1)
            pool.iota(kept.iota[:], pattern=[[1, P]], base=0, channel_multiplier=0,
                      allow_small_or_imprecise_dtypes=True).then_inc(masks_ready, 1)
            pool.iota(kept.spare[:], pattern=[[1, 1]], base=s.nodes, channel_multiplier=1,
                      allow_small_or_imprecise_dtypes=True).then_inc(masks_ready, 1)

        @block.vector
        def _(dve):
            dve.memset(zeros[:], 0.0).then_inc(zeros_set, 1)
            dve.memset(kept.src_f[:, s.cols:], 0.0).then_inc(floats_ready, 1)
            dve.wait_ge(indices_loaded, 32)
            dve.tensor_copy(kept.src_f[:, 0:s.cols], src_i[:]).then_inc(floats_ready, 1)
            dve.tensor_copy(kept.dst_f[:], dst_i[:]).then_inc(floats_ready, 1)
            dve.wait_ge(floats_ready, 3)
            firsts = kept.dst_f[0:1, :].rearrange("p (g k) -> p g k", k=COLS)[:, :, 0]
            dve.tensor_scalar(base_f[:], firsts, float(s.nodes - WIN), 0.0, ALU.min, ALU.max).then_inc(base_ready, 1)
            dve.wait_ge(base_ready, 1)
            dve.tensor_copy(kept.base[:], base_f[:]).then_inc(base_ready, 1)
            dve.wait_ge(base_spread, 1)
            dve.tensor_tensor(kept.rel[:].rearrange("p (g k) -> p g k", k=COLS),
                              kept.dst_f[:].rearrange("p (g k) -> p g k", k=COLS),
                              ps_base[:, 0:s.groups].unsqueeze(2).to_broadcast([P, s.groups, COLS]),
                              ALU.subtract).then_inc(rel_ready, 1)
            dve.wait_ge(rel_ready, 1)
            dve.tensor_scalar(under[:], kept.rel[:], 0.0, None, ALU.is_lt).then_inc(marks_ready, 1)
            dve.tensor_scalar(over[:], kept.rel[:], float(WIN - 1), None, ALU.is_gt).then_inc(marks_ready, 1)
            dve.wait_ge(marks_ready, 2)
            dve.tensor_tensor(under[:], under[:], over[:], ALU.add).then_inc(marks_joined, 1)
            dve.wait_ge(marks_joined, 1)
            dve.reduce_sum(count[:], under[:], AX.X).then_inc(count_ready, 1)
            dve.wait_ge(total_ready, 1)
            dve.tensor_scalar(kept.outside[:], ps_count[0:1, 0:1], float(-s.pads), None, ALU.add).then_inc(finished, 1)
            dve.wait_ge(gamma_spread, 1)
            dve.tensor_copy(kept.gamma_all[:], ps_gamma[:, 0:P]).then_inc(finished, 1)
            dve.tensor_copy(kept.beta_all[:], ps_gamma[:, P:2 * P]).then_inc(finished, 1)
            dve.wait_ge(finished, 3)

        @block.tensor
        def _(pe):
            pe.wait_ge(consts_set, 3)
            pe.wait_ge(base_ready, 1)
            pe.matmul(ps_base[:, 0:s.groups], kept.ones[0:1, :], base_f[:], start=True, stop=True).then_inc(base_spread, 1)
            pe.wait_ge(count_ready, 1)
            pe.matmul(ps_count[0:1, 0:1], count[:], kept.ones[:, 0:1], start=True, stop=True).then_inc(total_ready, 1)
            pe.wait_ge(weights_loaded, 16 * 9)
            pe.matmul(ps_gamma[:, 0:P], kept.ones[0:1, :], kept.gamma[:], start=True, stop=True)
            pe.matmul(ps_gamma[:, P:2 * P], kept.ones[0:1, :], kept.beta[:], start=True, stop=True).then_inc(gamma_spread, 1)


def load_edge_group(sp, s, edge_attr, out, g, loaded, lots_loaded):
    if not isinstance(g, int) or g < s.groups - 1:
        rows = edge_attr[bass.ds(g * GROUP, GROUP), :].rearrange("(p k) f -> p (k f)", p=P)
        sp.dma_start(out, rows).then_inc(loaded, 16)
        return
    whole, part = divmod(s.tail, COLS)
    used = part * s.feat
    last = edge_attr[g * GROUP:s.edges, :]
    other = edge_attr[0:GROUP, :].rearrange("(p k) f -> p (k f)", p=P)
    lots = [(out[0:whole, :], last[0:whole * COLS, :].rearrange("(p k) f -> p (k f)", k=COLS))]
    if part:
        lots += [(out[whole:whole + 1, 0:used], last[whole * COLS:s.tail, :].rearrange("(p k) f -> p (k f)", k=part)),
                 (out[whole:whole + 1, used:], other[whole:whole + 1, used:])]
    filled = whole + (part > 0)
    lots += [(out[filled:P, :], other[filled:P, :])]
    for to, rows in lots:
        sp.dma_start(to, rows).then_inc(lots_loaded, 16)
    sp.wait_ge(lots_loaded, 16 * len(lots))
    sp.sem_inc(loaded, 16)


def general_edges(nc, s, kept, name, rows_from, gather_at, limit, scatter_at, edge_attr, table):
    with ExitStack() as ctx:
        sb, ps, sem = allocator(nc, ctx)
        index = sb(f"{name}_index", [P, 1], I32)
        rows = sb(f"{name}_rows", [P, P])
        attr = sb(f"{name}_attr", [P, COLS * P])
        value = sb(f"{name}_value", [P, P])
        same = sb(f"{name}_same", [P, P])
        repeat = sb(f"{name}_repeat", [P, P])
        repeats = sb(f"{name}_repeats", [P, 1])
        to = sb(f"{name}_to", [P, 1])
        step = sb(f"{name}_step", [P, 1])
        target = sb(f"{name}_target", [P, 1], I32)
        summed = sb(f"{name}_summed", [P, P])
        ps_at = ps(f"{name}_ps_at", [P, 512])
        ps_sum = ps(f"{name}_ps_sum", [P, 512])
        index_ready = sem(f"{name}_index_ready")
        rows_gathered = sem(f"{name}_rows_gathered")
        attr_loaded = sem(f"{name}_attr_loaded")
        lots_loaded = sem(f"{name}_lots_loaded")
        to_ready = sem(f"{name}_to_ready")
        at_spread = sem(f"{name}_at_spread")
        same_ready = sem(f"{name}_same_ready")
        repeat_ready = sem(f"{name}_repeat_ready")
        repeats_ready = sem(f"{name}_repeats_ready")
        step_ready = sem(f"{name}_step_ready")
        target_ready = sem(f"{name}_target_ready")
        value_ready = sem(f"{name}_value_ready")
        sum_ready = sem(f"{name}_sum_ready")
        summed_ready = sem(f"{name}_summed_ready")
        rows_added = sem(f"{name}_rows_added")
        block = ctx.enter_context(nc.Block())

        @block.sync
        def _(sp):
            if edge_attr is not None:
                with sp.Fori(0, s.groups - 1) as g:
                    load_edge_group(sp, s, edge_attr, attr[:], g, attr_loaded, lots_loaded)
                    sp.wait_ge(value_ready, g * COLS + COLS)
                    passed(sp, kept)
                load_edge_group(sp, s, edge_attr, attr[:], s.groups - 1, attr_loaded, lots_loaded)

        @block.gpsimd
        def _(pool):
            with pool.Fori(0, s.groups) as g:
                for k in range(COLS):
                    n = g * COLS + (k + 1)
                    pool.wait_ge(index_ready, n)
                    passed(pool, kept)
                    pool.indirect_dma_start(rows[:], None, rows_from, bass.IndirectOffsetOnAxis(index[:, 0:1], 0)).then_inc(rows_gathered, 16)
                    pool.wait_ge(target_ready, n)
                    passed(pool, kept)
                    pool.wait_ge(summed_ready, n)
                    passed(pool, kept)
                    pool.indirect_dma_start(table, bass.IndirectOffsetOnAxis(target[:, 0:1], 0), summed[:], None,
                                            compute_op=ALU.add).then_inc(rows_added, 16)
                    pool.wait_ge(rows_added, n * 16)
                    passed(pool, kept)

        @block.vector
        def _(dve):
            with dve.Fori(0, s.groups) as g:
                if edge_attr is not None:
                    dve.wait_ge(attr_loaded, g * 16 + 16)
                    passed(dve, kept)
                for k in range(COLS):
                    n = g * COLS + (k + 1)
                    col = bass.ds(g * COLS + k, 1)
                    dve.tensor_scalar(index[:], gather_at[:, col], float(limit), None, ALU.min).then_inc(index_ready, 1)
                    dve.tensor_scalar(to[:], scatter_at[:, col], float(s.nodes), None, ALU.min).then_inc(to_ready, 1)
                    dve.wait_ge(at_spread, n)
                    dve.tensor_scalar(same[:], ps_at[:, 0:P], to[:], None, ALU.is_equal).then_inc(same_ready, 1)
                    dve.wait_ge(same_ready, n)
                    dve.tensor_tensor(repeat[:], same[:], kept.earlier[:], ALU.mult).then_inc(repeat_ready, 1)
                    dve.wait_ge(repeat_ready, n)
                    dve.reduce_max(repeats[:], repeat[:], AX.X).then_inc(repeats_ready, 1)
                    dve.wait_ge(repeats_ready, n)
                    dve.scalar_tensor_tensor(out=step[:], in0=kept.spare[:], scalar=to[:], in1=repeats[:],
                                             op0=ALU.subtract, op1=ALU.mult).then_inc(step_ready, 1)
                    dve.wait_ge(step_ready, n)
                    dve.tensor_tensor(target[:], step[:], to[:], ALU.add).then_inc(target_ready, 1)
                    dve.wait_ge(rows_gathered, n * 16)
                    if edge_attr is None:
                        dve.tensor_scalar(value[:], rows[:], kept.weight[:, col], None, ALU.mult).then_inc(value_ready, 1)
                    else:
                        dve.tensor_tensor(value[:], rows[:], attr[:, k * P:(k + 1) * P], ALU.add).then_inc(value_ready, 1)
                    dve.wait_ge(rows_added, n * 16)
                    passed(dve, kept)

        @block.tensor
        def _(pe):
            with pe.Fori(0, s.groups) as g:
                for k in range(COLS):
                    n = g * COLS + (k + 1)
                    pe.wait_ge(to_ready, n)
                    pe.matmul(ps_at[:, 0:P], to[:].to_broadcast([P, P]), kept.ident[:], start=True, stop=True).then_inc(at_spread, 1)
                    pe.wait_ge(value_ready, n)
                    pe.matmul(ps_sum[:, 0:P], same[:], value[:], start=True, stop=True).then_inc(sum_ready, 1)

        @block.scalar
        def _(act):
            with act.Fori(0, s.groups) as g:
                for k in range(COLS):
                    n = g * COLS + (k + 1)
                    act.wait_ge(sum_ready, n)
                    act.activation(summed[:], ps_sum[:, 0:P], ACT.Copy).then_inc(summed_ready, 1)


def norm_steps(dve, kept, names, x, stats, both, sq, rs, n):
    raise NotImplementedError


def first_norm(nc, s, kept, x, x1_sb, tables, x1_rows):
    T = len(tables)
    with ExitStack() as ctx:
        sb, ps, sem = allocator(nc, ctx)
        part = sb("part", [P, 2, T, HALF, P])
        xin = sb("xin", [P, 2, HALF, P])
        axt = sb("axt", [P, HALF * P])
        h = sb("h", [P, HALF, P])
        stats = sb("stats1", [P, HALF, 6])
        both = sb("both1", [P, HALF, 2])
        sd = sb("sd1", [P, HALF])
        rsd = sb("rsd1", [P, HALF])
        ps_axt = [ps(f"ps_axt{i}", [P, HALF * P]) for i in range(2)]
        ps_out = [ps(f"ps_out{i}", [P, HALF * P]) for i in range(2)]
        in_loaded = [sem(f"in_loaded{i}") for i in range(2)]
        axt_summed = sem("axt_summed")
        axt_ready = sem("axt_ready")
        out_ready = sem("out_ready")
        h_ready = sem("h_ready")
        stats_ready = sem("stats_ready1")
        both_ready = sem("both_ready1")
        sd_ready = sem("sd_ready1")
        rsd_ready = sem("rsd_ready1")
        x1_ready = sem("x1_ready")
        x1_stored = sem("x1_stored")
        block = ctx.enter_context(nc.Block())
        last = s.nodes - s.chunk

        def start(c):
            return last if isinstance(c, int) and c == s.chunks - 1 else c * s.chunk

        def rows(table, c):
            return table[bass.ds(start(c), s.chunk), :].rearrange("(t p) f -> p t f", p=P)

        def each(engine, one):
            assert s.chunks % 2
            with engine.Fori(0, s.chunks // 2) as j:
                one(j * 2, 0)
                one(j * 2 + 1, 1)
            one(s.chunks - 1, 0)

        @block.sync
        def _(sp):
            def load(c, u, free):
                if free is not None:
                    sp.wait_ge(axt_summed, free)
                    passed(sp, kept)
                    sp.wait_ge(h_ready, free)
                    passed(sp, kept)
                for t in range(T):
                    sp.dma_start(part[:, u, t], rows(tables[t], c)).then_inc(in_loaded[u], 16)
                sp.dma_start(xin[:, u], rows(x, c)).then_inc(in_loaded[u], 16)
            load(0, 0, None)
            load(1, 1, None)
            with sp.Fori(1, s.chunks // 2) as j:
                load(j * 2, 0, j * 2 - 1)
                load(j * 2 + 1, 1, j * 2)
            load(s.chunks - 1, 0, s.chunks - 2)

        @block.tensor
        def _(pe):
            pe.sem_inc(kept.turn)

            def one(c, u):
                lot = 16 * (T + 1)
                pe.wait_ge(in_loaded[u], (c - u) * (lot // 2) + lot)
                for t in range(HALF):
                    for k in range(T):
                        done = pe.matmul(ps_axt[u][:, t * P:(t + 1) * P], part[:, u, k, t, :], kept.ident[:],
                                         start=k == 0, stop=k == T - 1)
                done.then_inc(axt_summed, 1)
                pe.wait_ge(axt_ready, c + 1)
                for t in range(HALF):
                    pe.matmul(ps_out[u][:, t * P:(t + 1) * P], axt[:, t * P:(t + 1) * P], kept.w[:], start=True, stop=False)
                    done = pe.matmul(ps_out[u][:, t * P:(t + 1) * P], kept.ones[0:1, :], kept.b[:], start=False, stop=True)
                done.then_inc(out_ready, 1)
            each(pe, one)

        @block.scalar
        def _(act):
            def one(c, u):
                act.wait_ge(axt_summed, c + 1)
                act.activation(axt[:], ps_axt[u][:], ACT.Copy).then_inc(axt_ready, 1)
                act.wait_ge(both_ready, c * HALF + HALF)
                act.activation(sd[:], both[:, :, 1], ACT.Sqrt, bias=kept.eps[:]).then_inc(sd_ready, 1)
            each(act, one)

        @block.vector
        def _(dve):
            def one(c, u):
                dve.wait_ge(out_ready, c + 1)
                dve.tensor_tensor(h[:], ps_out[u][:].rearrange("p (t f) -> p t f", f=P), xin[:, u], ALU.add).then_inc(h_ready, 1)
                dve.wait_ge(h_ready, c + 1)
                passed(dve, kept)
                for t in range(HALF):
                    dve.bn_stats(stats[:, t, :], h[:, t, :]).then_inc(stats_ready, 1)
                dve.wait_ge(stats_ready, c * HALF + HALF)
                passed(dve, kept)
                for t in range(HALF):
                    dve.bn_aggr(both[:, t, :], stats[:, t, :]).then_inc(both_ready, 1)
                dve.wait_ge(sd_ready, c + 1)
                dve.reciprocal(rsd[:], sd[:]).then_inc(rsd_ready, 1)
                dve.wait_ge(rsd_ready, c + 1)
                passed(dve, kept)
                for t in range(HALF):
                    out = x1_sb[:, bass.ds(c * HALF + t, 1), :].rearrange("p t f -> p (t f)")
                    dve.tensor_scalar(out, h[:, t, :], both[:, t, 0:1], rsd[:, t:t + 1],
                                      ALU.subtract, ALU.mult).then_inc(x1_ready, 1)
                dve.wait_ge(x1_ready, c * HALF + HALF)
                passed(dve, kept)
            each(dve, one)

        @block.gpsimd
        def _(pool):
            def one(c, u):
                pool.wait_ge(x1_ready, c * HALF + HALF)
                passed(pool, kept)
                if isinstance(c, int):
                    pool.wait_ge(x1_stored, 16 * c)
                pool.dma_start(rows(x1_rows, c), x1_sb[:, bass.ds(c * HALF, HALF), :]).then_inc(x1_stored, 16)
            each(pool, one)
            pool.wait_ge(x1_stored, 16 * s.chunks)


def perceptron(nc, s, kept, ut, x1_sb, out):
    J = s.hidden // P
    with ExitStack() as ctx:
        sb, ps, sem = allocator(nc, ctx)
        hid = sb("hid", [P, J, s.chunk])
        h = sb("h2", [P, HALF, P])
        g = sb("g2", [P, HALF, P])
        y = sb("y2", [P, 2, HALF, P])
        stats = sb("stats2", [P, 2, HALF, 6])
        both = sb("both2", [P, 2, HALF, 2])
        sd = sb("sd2", [P, 2, HALF])
        rsd = sb("rsd2", [P, 2, HALF])
        ps_hid = [ps(f"ps_hid{i}", [P, s.chunk]) for i in range(4)]
        ps_out = [ps(f"ps_mlp{i}", [P, s.chunk]) for i in range(2)]
        hid_ready = sem("hid_ready")
        relu_ready = sem("relu_ready")
        mlp_ready = sem("mlp_ready")
        h_ready = sem("h2_ready")
        stats_ready = [sem(f"stats_ready2{i}") for i in range(2)]
        both_ready = [sem(f"both_ready2{i}") for i in range(2)]
        sd_ready = [sem(f"sd_ready2{i}") for i in range(2)]
        rsd_ready = [sem(f"rsd_ready2{i}") for i in range(2)]
        normed = sem("normed")
        scaled = sem("scaled")
        shifted = sem("shifted")
        joined = sem("joined")
        y_ready = sem("y_ready")
        y_stored = [sem(f"y_stored{i}") for i in range(2)]
        block = ctx.enter_context(nc.Block())

        def start(c):
            return s.nodes - s.chunk if isinstance(c, int) and c == s.chunks - 1 else c * s.chunk

        def each(engine, one):
            with engine.Fori(0, s.chunks // 2) as j:
                one(j * 2, 0)
                one(j * 2 + 1, 1)
            one(s.chunks - 1, 0)

        @block.tensor
        def _(pe):
            def one(c, u):
                for j in range(J):
                    done = pe.matmul(ps_hid[j][:], kept.w1[:, j * P:(j + 1) * P], ut[:, bass.ds(start(c), s.chunk)],
                                     start=True, stop=True)
                    done.then_inc(hid_ready, 1)
                pe.wait_ge(relu_ready, c * J + J)
                for t in range(HALF):
                    for j in range(J):
                        pe.matmul(ps_out[u][:, t * P:(t + 1) * P], hid[:, j, t * P:(t + 1) * P], kept.w2[:, j, :],
                                  start=j == 0, stop=False)
                    done = pe.matmul(ps_out[u][:, t * P:(t + 1) * P], kept.ones[0:1, :], kept.b2[:], start=False, stop=True)
                done.then_inc(mlp_ready, 1)
            each(pe, one)

        @block.scalar
        def _(act):
            act.sem_inc(mlp_ready, 1)

            def one(c, u):
                act.wait_ge(mlp_ready, c + 1)
                for j in range(J):
                    act.wait_ge(hid_ready, c * J + (j + 1))
                    act.activation(hid[:, j, :], ps_hid[j][:], ACT.Relu, bias=kept.b1[:, j:j + 1]).then_inc(relu_ready, 1)
                for i in range(2):
                    act.wait_ge(both_ready[i], c * HALF + HALF)
                    act.activation(sd[:, i, :], both[:, i, :, 1], ACT.Sqrt, bias=kept.eps[:]).then_inc(sd_ready[i], 1)
            each(act, one)

        @block.vector
        def _(dve):
            def norm(i, c, u, value, out, done):
                for t in range(HALF):
                    dve.bn_stats(stats[:, i, t, :], value[:, t, :]).then_inc(stats_ready[i], 1)
                dve.wait_ge(stats_ready[i], c * HALF + HALF)
                passed(dve, kept)
                for t in range(HALF):
                    dve.bn_aggr(both[:, i, t, :], stats[:, i, t, :]).then_inc(both_ready[i], 1)
                dve.wait_ge(sd_ready[i], c + 1)
                dve.reciprocal(rsd[:, i, :], sd[:, i, :]).then_inc(rsd_ready[i], 1)
                dve.wait_ge(rsd_ready[i], c + 1)
                passed(dve, kept)
                for t in range(HALF):
                    dve.tensor_scalar(out[:, t, :], value[:, t, :], both[:, i, t, 0:1], rsd[:, i, t:t + 1],
                                      ALU.subtract, ALU.mult).then_inc(done, 1)

            def one(c, u):
                own = x1_sb[:, bass.ds(c * HALF, HALF), :]
                dve.wait_ge(mlp_ready, c + 2)
                dve.tensor_tensor(h[:], ps_out[u][:].rearrange("p (t f) -> p t f", f=P), own, ALU.add).then_inc(h_ready, 1)
                dve.wait_ge(h_ready, c + 1)
                passed(dve, kept)
                norm(0, c, u, h, g, normed)
                dve.wait_ge(normed, c * HALF + HALF)
                dve.tensor_tensor(g[:], g[:], kept.gamma_all[:].unsqueeze(1).to_broadcast([P, HALF, P]), ALU.mult).then_inc(scaled, 1)
                dve.wait_ge(scaled, c + 1)
                dve.tensor_tensor(g[:], g[:], kept.beta_all[:].unsqueeze(1).to_broadcast([P, HALF, P]), ALU.add).then_inc(shifted, 1)
                dve.wait_ge(shifted, c + 1)
                dve.tensor_tensor(h[:], g[:], own, ALU.add).then_inc(joined, 1)
                dve.wait_ge(joined, c + 1)
                passed(dve, kept)
                dve.wait_ge(y_stored[u], (c - u) * 8 + 16)
                passed(dve, kept)
                norm(1, c, u, h, y[:, u], y_ready)
                dve.wait_ge(y_ready, c * HALF + HALF)
                passed(dve, kept)
            each(dve, one)

        @block.sync
        def _(sp):
            sp.sem_inc(y_stored[0], 16)
            sp.sem_inc(y_stored[1], 16)

            def one(c, u):
                sp.wait_ge(y_ready, c * HALF + HALF)
                passed(sp, kept)
                if isinstance(c, int):
                    sp.wait_ge(y_stored[1], 16 + 16 * (s.chunks // 2))
                sp.dma_start(out[bass.ds(start(c), s.chunk), :].rearrange("(t p) f -> p t f", p=P), y[:, u])\
                    .then_inc(y_stored[u], 16)
            each(sp, one)
            sp.wait_ge(y_stored[0], 16 + 16 * (s.chunks // 2 + 1))
            sp.wait_ge(y_stored[1], 16 + 16 * (s.chunks // 2))


def transposed_sums(nc, s, kept, u_table, ut):
    with ExitStack() as ctx:
        sb, ps, sem = allocator(nc, ctx)
        rows = sb("u_rows", [P, HALF, P])
        ps_t = ps("ps_ut", [P, s.chunk])
        rows_loaded = sem("u_rows_loaded")
        turned = sem("u_turned")
        copied = sem("u_copied")
        block = ctx.enter_context(nc.Block())

        def start(c):
            return s.nodes - s.chunk if isinstance(c, int) else c * s.chunk

        def each(engine, one):
            with engine.Fori(0, s.chunks - 1) as c:
                one(c)
            one(s.chunks - 1)

        @block.sync
        def _(sp):
            def one(c):
                sp.dma_start(rows[:], u_table[bass.ds(start(c), s.chunk), :].rearrange("(t p) f -> p t f", p=P)).then_inc(rows_loaded, 16)
                sp.wait_ge(copied, c + 1)
                passed(sp, kept)
            each(sp, one)

        @block.tensor
        def _(pe):
            def one(c):
                pe.wait_ge(rows_loaded, c * 16 + 16)
                for t in range(HALF):
                    done = pe.matmul(ps_t[:, t * P:(t + 1) * P], rows[:, t, :], kept.ident[:], start=True, stop=True)
                done.then_inc(turned, 1)
            each(pe, one)

        @block.vector
        def _(dve):
            def one(c):
                dve.wait_ge(turned, c + 1)
                passed(dve, kept)
                dve.tensor_copy(ut[:, bass.ds(start(c), s.chunk)], ps_t[:]).then_inc(copied, 1)
            each(dve, one)
            dve.wait_ge(copied, s.chunks)


def zero_table(nc, s, table):
    with ExitStack() as ctx:
        sb, ps, sem = allocator(nc, ctx)
        zeros = sb("u_zeros", [P, s.rows])
        zeros_set = sem("u_zeros_set")
        zeroed = sem("u_zeroed")
        block = ctx.enter_context(nc.Block())

        @block.vector
        def _(dve):
            dve.memset(zeros[:], 0.0).then_inc(zeros_set, 1)

        @block.sync
        def _(sp):
            sp.wait_ge(zeros_set, 1)
            sp.dma_start(table.rearrange("(p c) f -> p (c f)", p=P), zeros[:]).then_inc(zeroed, 16)
            sp.wait_ge(zeroed, 16)


def gnn(nc, x, src, dst, edge_attr, weight, w, b, w1, b1, w2, b2, gamma, beta, out):
    s = Shapes(x, edge_attr, w1)
    scratch = lambda name: nc.dram_tensor(name, (s.rows, s.feat), F32, kind="Internal").ap()
    tables = [scratch(f"ax_part{t}") for t in range(TABLES)]
    x1_rows, u_table = scratch("x1_rows"), scratch("u_table")
    with ExitStack() as ctx:
        kept = Kept(nc, ctx, s)
        prepare(nc, s, kept, src, dst, weight, w, b, w1, b1, w2, b2, gamma, beta, [*tables, x1_rows])
        general_edges(nc, s, kept, "g0", x, kept.dst_f, s.nodes - 1, kept.src_f, None, tables[0])
        x1_sb = ctx.enter_context(nc.sbuf_tensor("x1_sb", [P, s.chunks * HALF, P], F32))
        first_norm(nc, s, kept, x, x1_sb, tables, x1_rows)
        ut = ctx.enter_context(nc.sbuf_tensor("ut", [P, s.nodes], F32))
        zero_table(nc, s, u_table)
        general_edges(nc, s, kept, "g1", x1_rows, kept.src_f, s.nodes, kept.dst_f, edge_attr, u_table)
        transposed_sums(nc, s, kept, u_table, ut)
        perceptron(nc, s, kept, ut, x1_sb, out)


def kernel(**inputs):
    import numpy as np
    import concourse.bacc as bacc
    from concourse.bass_utils import run_bass_kernel_spmd

    n, e = inputs["x"].shape[0], inputs["src"].shape[0]
    groups = 2 * -(-e // (2 * GROUP))

    def columns(a, pad):
        full = np.full(groups * GROUP, pad, np.asarray(a).dtype)
        full[:e] = a
        return np.ascontiguousarray(full.reshape(groups, P, COLS).transpose(1, 0, 2).reshape(P, groups * COLS))

    arrays = {
        "x": np.asarray(inputs["x"]),
        "src": columns(inputs["src"], n),
        "dst": columns(inputs["dst"], 2 * n),
        "edge_attr": np.asarray(inputs["edge_attr_128"]),
        "weight": columns(inputs["edge_weight"], 0),
        "w": np.asarray(inputs["L0_gnn_W"]),
        "b": np.asarray(inputs["L0_gnn_b"]).reshape(1, -1),
        "w1": np.asarray(inputs["L1_gnn_W1"]),
        "b1": np.ascontiguousarray(np.asarray(inputs["L1_gnn_b1"]).reshape(-1, P).T),
        "w2": np.asarray(inputs["L1_gnn_W2"]),
        "b2": np.asarray(inputs["L1_gnn_b2"]).reshape(1, -1),
        "gamma": np.asarray(inputs["L1_gnn_gamma"]).reshape(1, -1),
        "beta": np.asarray(inputs["L1_gnn_beta"]).reshape(1, -1),
    }
    nc = bacc.Bacc("TRN2", target_bir_lowering=False, num_devices=1)
    aps = [nc.dram_tensor(f"{k}_dram", a.shape, mybir.dt.from_np(a.dtype), kind="ExternalInput").ap()
           for k, a in arrays.items()]
    y = nc.dram_tensor("y_dram", arrays["x"].shape, F32, kind="ExternalOutput").ap()
    gnn(nc, *aps, y)
    result = run_bass_kernel_spmd(nc, [{f"{k}_dram": a for k, a in arrays.items()}], core_ids=[0])
    return result.results[0]["y_dram"]
```

```python
import concourse.bass as bass
from concourse import mybir
from contextlib import ExitStack

F32 = mybir.dt.float32
I32 = mybir.dt.int32
ALU = mybir.AluOpType
ACT = mybir.ActivationFunctionType
AX = mybir.AxisListType

P = 128
COLS = 8
GROUP = COLS * P
HALF = 4
WIN = 128
TABLES = 4
EPS = 1e-5


class Shapes:

    def __init__(self, x, edge_attr, w1):
        self.nodes, self.feat = x.shape
        self.edges = edge_attr.shape[0]
        self.hidden = w1.shape[1]
        assert self.feat == P and self.hidden % P == 0
        self.groups = 2 * -(-self.edges // (2 * GROUP))
        self.cols = self.groups * COLS
        self.pads = self.groups * GROUP - self.edges
        self.tail = self.edges - (self.groups - 1) * GROUP
        assert 0 < self.tail < GROUP
        self.rows = P * (-(-self.nodes // P) + 1)
        self.zero_repeats = next(n for n in range(8, 0, -1) if self.rows // P % n == 0)
        self.chunk = HALF * P
        self.chunks = -(-self.nodes // self.chunk)
        self.lag = self.groups // 2 - HALF * (self.chunks - 1)
        assert self.lag > 0


def allocator(nc, ctx, whole):
    sb = lambda name, shape, dt=F32: ctx.enter_context(nc.sbuf_tensor(name, shape, dt))
    ps = lambda name, shape: ctx.enter_context(nc.psum_tensor(name, shape, F32))
    sem = lambda name: whole.enter_context(nc.semaphore(name))
    return sb, ps, sem


class Kept:

    def __init__(self, nc, ctx, s):
        sb, _, self_sem = allocator(nc, ctx, ctx)
        self.whole = ctx
        self.ident = sb("ident", [P, P])
        self.ones = sb("ones", [P, P])
        self.earlier = sb("earlier", [P, P])
        self.iota = sb("iota", [P, P])
        self.spare = sb("spare", [P, 1])
        self.src_f = sb("src_f", [P, s.cols + 3 * HALF])
        self.dst_f = sb("dst_f", [P, s.cols])
        self.rel = sb("rel", [P, s.cols])
        self.weight = sb("weight", [P, s.cols])
        self.base = sb("base", [1, s.groups], I32)
        self.outside = sb("outside", [1, 1], I32)
        self.w = sb("w_sb", [P, P])
        self.b = sb("b_sb", [1, P])
        self.w1 = sb("w1_sb", [P, s.hidden])
        self.b1 = sb("b1_sb", [P, s.hidden // P])
        self.w2 = sb("w2_sb", [P, s.hidden // P, P])
        self.b2 = sb("b2_sb", [1, P])
        self.gamma = sb("gamma_sb", [1, P])
        self.beta = sb("beta_sb", [1, P])
        self.gamma_all = sb("gamma_all", [P, P])
        self.beta_all = sb("beta_all", [P, P])
        self.eps = sb("eps_sb", [P, 1])
        self.turn = self_sem("turn")


def passed(engine, kept):
    engine.sem_inc(kept.turn)


def prepare(nc, s, kept, src, dst, weight, w, b, w1, b1, w2, b2, gamma, beta, x1_rows):
    with ExitStack() as ctx:
        sb, ps, sem = allocator(nc, ctx, kept.whole)
        src_i = sb("src_i", [P, s.cols], I32)
        dst_i = sb("dst_i", [P, s.cols], I32)
        base_f = sb("base_f", [1, s.groups])
        under = sb("under", [P, s.cols])
        over = sb("over", [P, s.cols])
        count = sb("count", [P, 1])
        zeros = sb("zeros", [P, (s.rows - s.nodes) * s.feat // P])
        ps_base = ps("ps_base", [P, 512])
        ps_count = ps("ps_count", [P, 512])
        ps_gamma = ps("ps_gamma", [P, 512])
        consts_set = sem("consts_set")
        masks_ready = sem("masks_ready")
        indices_loaded = sem("indices_loaded")
        weights_loaded = sem("weights_loaded")
        zeros_set = sem("zeros_set")
        rows_zeroed = sem("rows_zeroed")
        floats_ready = sem("floats_ready")
        base_ready = sem("base_ready")
        base_spread = sem("base_spread")
        rel_ready = sem("rel_ready")
        marks_ready = sem("marks_ready")
        marks_joined = sem("marks_joined")
        count_ready = sem("count_ready")
        total_ready = sem("total_ready")
        least_ready = sem("least_ready")
        early_ready = sem("early_ready")
        least = sb("least", [1, s.groups])
        early = sb("early", [1, s.groups])
        early_count = sb("early_count", [1, 1])
        gamma_spread = sem("gamma_spread")
        finished = sem("finished")
        block = ctx.enter_context(nc.Block())

        @block.sync
        def _(sp):
            sp.dma_start(src_i[:], src).then_inc(indices_loaded, 16)
            sp.dma_start(dst_i[:], dst).then_inc(indices_loaded, 16)
            sp.dma_start(kept.weight[:], weight).then_inc(weights_loaded, 16)
            sp.dma_start(kept.w[:], w).then_inc(weights_loaded, 16)
            sp.dma_start(kept.w1[:], w1).then_inc(weights_loaded, 16)
            sp.dma_start(kept.w2[:], w2.rearrange("(j p) f -> p j f", p=P)).then_inc(weights_loaded, 16)
            sp.dma_start(kept.b1[:], b1).then_inc(weights_loaded, 16)
            for row, vector in ((kept.b, b), (kept.b2, b2), (kept.gamma, gamma), (kept.beta, beta)):
                sp.dma_start(row[:], vector).then_inc(weights_loaded, 16)
            sp.wait_ge(weights_loaded, 16 * 9)

        @block.scalar
        def _(act):
            act.wait_ge(zeros_set, 1)
            spare_rows = x1_rows[s.nodes:s.rows, :].rearrange("r f -> (r f)").rearrange("(p c) -> p c", p=P)
            act.dma_start(spare_rows, zeros[:]).then_inc(rows_zeroed, 16)
            act.wait_ge(rows_zeroed, 16)

        @block.gpsimd
        def _(pool):
            pool.memset(kept.ident[:], 0.0).then_inc(consts_set, 1)
            pool.memset(kept.ones[:], 1.0).then_inc(consts_set, 1)
            pool.memset(kept.eps[:], EPS).then_inc(consts_set, 1)
            pool.wait_ge(consts_set, 3)
            pool.affine_select(out=kept.ident[:], in_=kept.ident[:], compare_op=ALU.not_equal, fill=1.0,
                               base=0, pattern=[[-1, P]], channel_multiplier=1).then_inc(masks_ready, 1)
            pool.affine_select(out=kept.earlier[:], in_=kept.ones[:], compare_op=ALU.is_gt, fill=0.0,
                               base=0, pattern=[[-1, P]], channel_multiplier=1).then_inc(masks_ready, 1)
            pool.iota(kept.iota[:], pattern=[[1, P]], base=0, channel_multiplier=0,
                      allow_small_or_imprecise_dtypes=True).then_inc(masks_ready, 1)
            pool.iota(least[:].rearrange("p (j u) -> p j u", u=2), pattern=[[P, s.groups // 2], [0, 2]],
                      base=P * (1 - s.lag), channel_multiplier=0,
                      allow_small_or_imprecise_dtypes=True).then_inc(least_ready, 1)
            pool.iota(kept.spare[:], pattern=[[1, 1]], base=s.nodes, channel_multiplier=1,
                      allow_small_or_imprecise_dtypes=True).then_inc(masks_ready, 1)

        @block.vector
        def _(dve):
            dve.memset(zeros[:], 0.0).then_inc(zeros_set, 1)
            dve.memset(kept.src_f[:, s.cols:], 0.0).then_inc(floats_ready, 1)
            dve.wait_ge(indices_loaded, 32)
            dve.tensor_copy(kept.src_f[:, 0:s.cols], src_i[:]).then_inc(floats_ready, 1)
            dve.tensor_copy(kept.dst_f[:], dst_i[:]).then_inc(floats_ready, 1)
            dve.wait_ge(floats_ready, 3)
            firsts = kept.dst_f[0:1, :].rearrange("p (g k) -> p g k", k=COLS)[:, :, 0]
            dve.tensor_scalar(base_f[:], firsts, float(s.nodes - WIN), 0.0, ALU.min, ALU.max).then_inc(base_ready, 1)
            dve.wait_ge(base_ready, 1)
            dve.tensor_copy(kept.base[:], base_f[:]).then_inc(base_ready, 1)
            dve.wait_ge(base_spread, 1)
            dve.tensor_tensor(kept.rel[:].rearrange("p (g k) -> p g k", k=COLS),
                              kept.dst_f[:].rearrange("p (g k) -> p g k", k=COLS),
                              ps_base[:, 0:s.groups].unsqueeze(2).to_broadcast([P, s.groups, COLS]),
                              ALU.subtract).then_inc(rel_ready, 1)
            dve.wait_ge(rel_ready, 1)
            dve.tensor_scalar(under[:], kept.rel[:], 0.0, None, ALU.is_lt).then_inc(marks_ready, 1)
            dve.tensor_scalar(over[:], kept.rel[:], float(WIN - 1), None, ALU.is_gt).then_inc(marks_ready, 1)
            dve.wait_ge(marks_ready, 2)
            dve.tensor_tensor(under[:], under[:], over[:], ALU.add).then_inc(marks_joined, 1)
            dve.wait_ge(marks_joined, 1)
            dve.reduce_sum(count[:], under[:], AX.X).then_inc(count_ready, 1)
            dve.wait_ge(least_ready, 1)
            dve.tensor_tensor(early[:], base_f[:], least[:], ALU.is_lt).then_inc(early_ready, 1)
            dve.wait_ge(early_ready, 1)
            dve.reduce_sum(early_count[:], early[:], AX.X).then_inc(early_ready, 1)
            dve.wait_ge(early_ready, 2)
            dve.wait_ge(total_ready, 1)
            dve.scalar_tensor_tensor(out=kept.outside[:], in0=ps_count[0:1, 0:1], scalar=float(-s.pads),
                                     in1=early_count[:], op0=ALU.add, op1=ALU.add).then_inc(finished, 1)
            dve.wait_ge(gamma_spread, 1)
            dve.tensor_copy(kept.gamma_all[:], ps_gamma[:, 0:P]).then_inc(finished, 1)
            dve.tensor_copy(kept.beta_all[:], ps_gamma[:, P:2 * P]).then_inc(finished, 1)
            dve.wait_ge(finished, 3)

        @block.tensor
        def _(pe):
            pe.wait_ge(consts_set, 3)
            pe.wait_ge(base_ready, 1)
            pe.matmul(ps_base[:, 0:s.groups], kept.ones[0:1, :], base_f[:], start=True, stop=True).then_inc(base_spread, 1)
            pe.wait_ge(count_ready, 1)
            pe.matmul(ps_count[0:1, 0:1], count[:], kept.ones[:, 0:1], start=True, stop=True).then_inc(total_ready, 1)
            pe.wait_ge(weights_loaded, 16 * 9)
            pe.matmul(ps_gamma[:, 0:P], kept.ones[0:1, :], kept.gamma[:], start=True, stop=True)
            pe.matmul(ps_gamma[:, P:2 * P], kept.ones[0:1, :], kept.beta[:], start=True, stop=True).then_inc(gamma_spread, 1)


def load_edge_group(sp, s, edge_attr, out, g, loaded, lots_loaded):
    if not isinstance(g, int) or g < s.groups - 1:
        rows = edge_attr[bass.ds(g * GROUP, GROUP), :].rearrange("(p k) f -> p (k f)", p=P)
        sp.dma_start(out, rows).then_inc(loaded, 16)
        return
    whole, part = divmod(s.tail, COLS)
    used = part * s.feat
    last = edge_attr[g * GROUP:s.edges, :]
    other = edge_attr[0:GROUP, :].rearrange("(p k) f -> p (k f)", p=P)
    lots = [(out[0:whole, :], last[0:whole * COLS, :].rearrange("(p k) f -> p (k f)", k=COLS))]
    if part:
        lots += [(out[whole:whole + 1, 0:used], last[whole * COLS:s.tail, :].rearrange("(p k) f -> p (k f)", k=part)),
                 (out[whole:whole + 1, used:], other[whole:whole + 1, used:])]
    filled = whole + (part > 0)
    lots += [(out[filled:P, :], other[filled:P, :])]
    for to, rows in lots:
        sp.dma_start(to, rows).then_inc(lots_loaded, 16)
    sp.wait_ge(lots_loaded, 16 * len(lots))
    sp.sem_inc(loaded, 16)


def general_edges(nc, s, kept, name, rows_from, gather_at, limit, scatter_at, edge_attr, table):
    with ExitStack() as ctx:
        sb, ps, sem = allocator(nc, ctx, kept.whole)
        index = sb(f"{name}_index", [P, 1], I32)
        rows = sb(f"{name}_rows", [P, P])
        attr = sb(f"{name}_attr", [P, COLS * P])
        value = sb(f"{name}_value", [P, P])
        same = sb(f"{name}_same", [P, P])
        repeat = sb(f"{name}_repeat", [P, P])
        repeats = sb(f"{name}_repeats", [P, 1])
        to = sb(f"{name}_to", [P, 1])
        step = sb(f"{name}_step", [P, 1])
        target = sb(f"{name}_target", [P, 1], I32)
        summed = sb(f"{name}_summed", [P, P])
        ps_at = ps(f"{name}_ps_at", [P, 512])
        ps_sum = ps(f"{name}_ps_sum", [P, 512])
        index_ready = sem(f"{name}_index_ready")
        rows_gathered = sem(f"{name}_rows_gathered")
        attr_loaded = sem(f"{name}_attr_loaded")
        lots_loaded = sem(f"{name}_lots_loaded")
        to_ready = sem(f"{name}_to_ready")
        at_spread = sem(f"{name}_at_spread")
        same_ready = sem(f"{name}_same_ready")
        repeat_ready = sem(f"{name}_repeat_ready")
        repeats_ready = sem(f"{name}_repeats_ready")
        step_ready = sem(f"{name}_step_ready")
        target_ready = sem(f"{name}_target_ready")
        value_ready = sem(f"{name}_value_ready")
        sum_ready = sem(f"{name}_sum_ready")
        summed_ready = sem(f"{name}_summed_ready")
        rows_added = sem(f"{name}_rows_added")
        block = ctx.enter_context(nc.Block())

        @block.sync
        def _(sp):
            if edge_attr is not None:
                with sp.Fori(0, s.groups - 1) as g:
                    load_edge_group(sp, s, edge_attr, attr[:], g, attr_loaded, lots_loaded)
                    sp.wait_ge(value_ready, g * COLS + COLS)
                    passed(sp, kept)
                load_edge_group(sp, s, edge_attr, attr[:], s.groups - 1, attr_loaded, lots_loaded)

        @block.gpsimd
        def _(pool):
            with pool.Fori(0, s.groups) as g:
                for k in range(COLS):
                    n = g * COLS + (k + 1)
                    pool.wait_ge(index_ready, n)
                    passed(pool, kept)
                    pool.indirect_dma_start(rows[:], None, rows_from, bass.IndirectOffsetOnAxis(index[:, 0:1], 0)).then_inc(rows_gathered, 16)
                    pool.wait_ge(target_ready, n)
                    passed(pool, kept)
                    pool.wait_ge(summed_ready, n)
                    passed(pool, kept)
                    pool.indirect_dma_start(table, bass.IndirectOffsetOnAxis(target[:, 0:1], 0), summed[:], None,
                                            compute_op=ALU.add).then_inc(rows_added, 16)
                    pool.wait_ge(rows_added, n * 16)
                    passed(pool, kept)

        @block.vector
        def _(dve):
            with dve.Fori(0, s.groups) as g:
                if edge_attr is not None:
                    dve.wait_ge(attr_loaded, g * 16 + 16)
                    passed(dve, kept)
                for k in range(COLS):
                    n = g * COLS + (k + 1)
                    col = bass.ds(g * COLS + k, 1)
                    dve.tensor_scalar(index[:], gather_at[:, col], float(limit), None, ALU.min).then_inc(index_ready, 1)
                    dve.tensor_scalar(to[:], scatter_at[:, col], float(s.nodes), None, ALU.min).then_inc(to_ready, 1)
                    dve.wait_ge(at_spread, n)
                    dve.tensor_scalar(same[:], ps_at[:, 0:P], to[:], None, ALU.is_equal).then_inc(same_ready, 1)
                    dve.wait_ge(same_ready, n)
                    dve.tensor_tensor(repeat[:], same[:], kept.earlier[:], ALU.mult).then_inc(repeat_ready, 1)
                    dve.wait_ge(repeat_ready, n)
                    dve.reduce_max(repeats[:], repeat[:], AX.X).then_inc(repeats_ready, 1)
                    dve.wait_ge(repeats_ready, n)
                    dve.scalar_tensor_tensor(out=step[:], in0=kept.spare[:], scalar=to[:], in1=repeats[:],
                                             op0=ALU.subtract, op1=ALU.mult).then_inc(step_ready, 1)
                    dve.wait_ge(step_ready, n)
                    dve.tensor_tensor(target[:], step[:], to[:], ALU.add).then_inc(target_ready, 1)
                    dve.wait_ge(rows_gathered, n * 16)
                    if edge_attr is None:
                        dve.tensor_scalar(value[:], rows[:], kept.weight[:, col], None, ALU.mult).then_inc(value_ready, 1)
                    else:
                        dve.tensor_tensor(value[:], rows[:], attr[:, k * P:(k + 1) * P], ALU.add).then_inc(value_ready, 1)
                    dve.wait_ge(rows_added, n * 16)
                    passed(dve, kept)

        @block.tensor
        def _(pe):
            with pe.Fori(0, s.groups) as g:
                for k in range(COLS):
                    n = g * COLS + (k + 1)
                    pe.wait_ge(to_ready, n)
                    pe.matmul(ps_at[:, 0:P], to[:].to_broadcast([P, P]), kept.ident[:], start=True, stop=True).then_inc(at_spread, 1)
                    pe.wait_ge(value_ready, n)
                    pe.matmul(ps_sum[:, 0:P], same[:], value[:], start=True, stop=True).then_inc(sum_ready, 1)

        @block.scalar
        def _(act):
            with act.Fori(0, s.groups) as g:
                for k in range(COLS):
                    n = g * COLS + (k + 1)
                    act.wait_ge(sum_ready, n)
                    act.activation(summed[:], ps_sum[:, 0:P], ACT.Copy).then_inc(summed_ready, 1)


def scatter_edges(nc, s, kept, x, tables):
    halves = 2 * s.groups
    with ExitStack() as ctx:
        sb, ps, sem = allocator(nc, ctx, kept.whole)
        zeros = sb("s_zeros", [P, s.rows // s.zero_repeats])
        window = sb("s_window", [P, 2, P])
        at = sb("s_at", [P, 2, HALF])
        hot = sb("s_hot", [P, 2, HALF, WIN])
        same = sb("s_same", [P, 2, HALF, P])
        repeat = sb("s_repeat", [P, HALF, P])
        repeats = sb("s_repeats", [P, HALF])
        back = sb("s_back", [P, HALF])
        target = sb("s_target", [P, 4, HALF], I32)
        mixed = sb("s_mixed", [P, 2, HALF, P])
        rows = sb("s_rows", [P, 4, HALF, P])
        ps_at = [ps(f"s_ps_at{i}", [P, HALF * P]) for i in range(2)]
        ps_mix = [ps(f"s_ps_mix{i}", [P, HALF * P]) for i in range(2)]
        ps_rows = [ps(f"s_ps_rows{i}", [P, HALF * P]) for i in range(2)]
        zeros_set = sem("s_zeros_set")
        window_loaded = [sem(f"s_window_loaded{i}") for i in range(2)]
        at_ready = sem("s_at_ready")
        at_spread = sem("s_at_spread")
        hot_ready = sem("s_hot_ready")
        same_ready = sem("s_same_ready")
        repeat_ready = sem("s_repeat_ready")
        repeats_ready = sem("s_repeats_ready")
        back_ready = sem("s_back_ready")
        target_ready = sem("s_target_ready")
        mix_summed = sem("s_mix_summed")
        mixed_ready = sem("s_mixed_ready")
        rows_summed = sem("s_rows_summed")
        rows_ready = sem("s_rows_ready")
        turns = sem("s_turns")
        added = [sem(f"s_added{t}") for t in range(TABLES)]
        block = ctx.enter_context(nc.Block())

        def steps(engine, one):
            with engine.Fori(0, s.groups // 2) as j:
                for u in range(2):
                    for h in range(2):
                        one(j, u, h, j * 4 + (2 * u + h))

        @block.sync
        def _(sp):
            with sp.Fori(0, s.groups // 2) as j:
                for u in range(2):
                    sp.wait_ge(rows_summed, j * 4 + (2 * u + 2))
                    passed(sp, kept)
                    first = sp.value_load(kept.base[0:1, bass.ds(j * 2 + u, 1)], min_val=0, max_val=s.nodes - WIN)
                    sp.dma_start(window[:, u, :], x[bass.ds(first, WIN), :]).then_inc(window_loaded[u], 16)

        @block.tensor
        def _(pe):
            pe.sem_inc(mix_summed, 2)
            pe.sem_inc(rows_summed, 4)
            pe.sem_inc(at_spread, 1)

            def spread(n, i):
                pe.wait_ge(at_ready, n + 1)
                for t in range(HALF):
                    done = pe.matmul(ps_at[i][:, t * P:(t + 1) * P], at[:, i, t:t + 1].to_broadcast([P, P]),
                                     kept.ident[:], start=True, stop=True)
                done.then_inc(at_spread, 1)

            def one(j, u, h, n):
                pe.wait_ge(hot_ready, n * HALF + HALF)
                pe.wait_ge(same_ready, n + 2)
                for t in range(HALF):
                    done = pe.matmul(ps_mix[h][:, t * P:(t + 1) * P], hot[:, h, t, :], same[:, h, t, :],
                                     start=True, stop=True)
                done.then_inc(mix_summed, 1)
                spread(n + 1, 1 - h)
                if h == 0:
                    pe.wait_ge(window_loaded[u], j * 16 + 16)
                pe.wait_ge(rows_ready, n + 1)
                pe.wait_ge(mixed_ready, n + 1)
                for t in range(HALF):
                    done = pe.matmul(ps_rows[h][:, t * P:(t + 1) * P], mixed[:, h, t, :], window[:, u, :],
                                     start=True, stop=True)
                done.then_inc(rows_summed, 1)
            spread(0, 0)
            steps(pe, one)

        @block.vector
        def _(dve):
            dve.sem_inc(same_ready, 1)
            dve.memset(zeros[:], 0.0).then_inc(zeros_set, 1)

            def one(j, u, h, n):
                q = 2 * u + h
                cols = bass.ds(n * HALF, HALF)
                dve.wait_ge(mix_summed, n + 1)
                for t in range(HALF):
                    col = bass.ds(n * HALF + t, 1)
                    dve.tensor_scalar(hot[:, h, t, :], kept.iota[:], kept.rel[:, col], kept.weight[:, col],
                                      ALU.is_equal, ALU.mult).then_inc(hot_ready, 1)
                dve.wait_ge(at_spread, n + 2)
                dve.tensor_tensor(same[:, h], ps_at[h][:].rearrange("p (t e) -> p t e", e=P),
                                  kept.src_f[:, cols].unsqueeze(2).to_broadcast([P, HALF, P]), ALU.is_equal).then_inc(same_ready, 1)
                dve.wait_ge(same_ready, n + 2)
                dve.tensor_tensor(repeat[:], same[:, h], kept.earlier[:].unsqueeze(1).to_broadcast([P, HALF, P]),
                                  ALU.mult).then_inc(repeat_ready, 1)
                dve.wait_ge(repeat_ready, n + 1)
                dve.reduce_max(repeats[:], repeat[:], AX.X).then_inc(repeats_ready, 1)
                dve.wait_ge(repeats_ready, n + 1)
                dve.scalar_tensor_tensor(out=back[:], in0=kept.src_f[:, cols], scalar=kept.spare[:], in1=repeats[:],
                                         op0=ALU.subtract, op1=ALU.mult).then_inc(back_ready, 1)
                dve.wait_ge(turns, n * HALF + HALF)
                dve.wait_ge(back_ready, n + 1)
                dve.tensor_tensor(target[:, q], kept.src_f[:, cols], back[:], ALU.subtract).then_inc(target_ready, 1)
            steps(dve, one)

        @block.scalar
        def _(act):
            act.sem_inc(rows_ready, 2)

            def take(n, i):
                act.activation(at[:, i, :], kept.src_f[:, bass.ds(n * HALF, HALF)], ACT.Copy).then_inc(at_ready, 1)
            take(0, 0)

            def one(j, u, h, n):
                act.wait_ge(at_spread, n + 1)
                passed(act, kept)
                take(n + 1, 1 - h)
                act.wait_ge(rows_summed, n + 3)
                act.wait_ge(mix_summed, n + 3)
                act.activation(mixed[:, h], ps_mix[h][:].rearrange("p (t e) -> p t e", e=P), ACT.Copy).then_inc(mixed_ready, 1)
                act.wait_ge(rows_summed, n + 5)
                act.wait_ge(turns, n * HALF + HALF)
                act.activation(rows[:, 2 * u + h], ps_rows[h][:].rearrange("p (t f) -> p t f", f=P), ACT.Copy).then_inc(rows_ready, 1)
            steps(act, one)

        @block.gpsimd
        def _(pool):
            pool.sem_inc(turns, 3 * HALF)
            pool.wait_ge(zeros_set, 1)
            for t in range(TABLES):
                pool.dma_start(tables[t].rearrange("(p r c) f -> p r (c f)", p=P, r=s.zero_repeats),
                               zeros[:].unsqueeze(1).to_broadcast([P, s.zero_repeats, s.rows // s.zero_repeats])).then_inc(added[t], 16)

            def one(j, u, h, n):
                q = 2 * u + h
                pool.wait_ge(rows_ready, n + 3)
                passed(pool, kept)
                pool.wait_ge(target_ready, n + 1)
                passed(pool, kept)
                for t in range(HALF):
                    pool.wait_ge(added[t], n * 16 + 16)
                    pool.sem_inc(turns, 1)
                    pool.indirect_dma_start(tables[t], bass.IndirectOffsetOnAxis(target[:, q, t:t + 1], 0), rows[:, q, t, :],
                                            None, compute_op=ALU.add).then_inc(added[t], 16)
            steps(pool, one)
            for t in range(TABLES):
                pool.wait_ge(added[t], 16 * (halves + 1))


def gather_edges(nc, s, kept, x1_rows, edge_attr, ut, x1_sb, out):
    J = s.hidden // P
    with ExitStack() as ctx:
        sb, ps, sem = allocator(nc, ctx, kept.whole)
        index = sb("r_index", [P, 4, HALF], I32)
        rows = sb("r_rows", [P, 4, HALF, P])
        attr = sb("r_attr", [P, 2, COLS * P])
        hot = sb("r_hot", [P, 2, HALF, WIN])
        ps_sum = [ps(f"r_ps_sum{i}", [P, HALF * P]) for i in range(2)]
        index_ready = sem("r_index_ready")
        rows_gathered = [sem(f"r_rows_gathered{i}") for i in range(4)]
        attr_loaded = [sem(f"r_attr_loaded{i}") for i in range(2)]
        lots_loaded = sem("r_lots_loaded")
        hot_ready = sem("r_hot_ready")
        used = sem("r_used")
        sums_cleared = sem("r_sums_cleared")
        sums_added = sem("r_sums_added")
        hid = sb("r_hid", [P, J, P])
        val = sb("r_val", [P, 2, P])
        unit = sb("r_unit", [P, P])
        y = sb("r_y", [P, P])
        stats = sb("r_stats", [P, 2, 6])
        both = sb("r_both", [P, 2, 2])
        sd = sb("r_sd", [P, 2])
        rsd = sb("r_rsd", [P, 2])
        ps_hid = ps("r_ps_hid", [P, J * P])
        ps_out = ps("r_ps_out", [P, 4 * P])
        hid_ready = sem("r_hid_ready")
        relu_ready = sem("r_relu_ready")
        mlp_ready = sem("r_mlp_ready")
        val_ready = [sem(f"r_val_ready{i}") for i in range(2)]
        stats_ready = [sem(f"r_stats_ready{i}") for i in range(2)]
        both_ready = [sem(f"r_both_ready{i}") for i in range(2)]
        sd_ready = [sem(f"r_sd_ready{i}") for i in range(2)]
        rsd_ready = [sem(f"r_rsd_ready{i}") for i in range(2)]
        unit_ready = sem("r_unit_ready")
        scaled = sem("r_scaled")
        shifted = sem("r_shifted")
        y_ready = sem("r_y_ready")
        y_stored = sem("r_y_stored")
        block = ctx.enter_context(nc.Block())

        def steps(engine, one, beside):
            def pair(j, block):
                for q in range(4):
                    one(j, q // 2, q % 2, j * 4 + q, (lambda: beside(q, *block)) if block else lambda: None)
            with engine.Fori(0, s.lag) as j:
                pair(j, None)
            with engine.Fori(s.lag, s.groups // 2) as j:
                i = j - s.lag
                pair(j, (i, i * P, i))
            left = -(-(s.nodes - (s.chunks - 1) * s.chunk) // P)
            for k in range(left):
                for q in range(4):
                    beside(q, s.groups // 2 - s.lag + k, s.nodes - (left - k) * P, s.chunks * HALF - left + k)

        @block.sync
        def _(sp):
            sp.sem_inc(y_stored, 16)

            def load(g, u):
                sp.wait_ge(used, g * 2 + 2)
                passed(sp, kept)
                load_edge_group(sp, s, edge_attr, attr[:, u], g, attr_loaded[u], lots_loaded)

            def store(i, first):
                sp.wait_ge(y_ready, i + 1)
                passed(sp, kept)
                if isinstance(i, int):
                    sp.wait_ge(y_stored, 16 * i + 16)
                sp.dma_start(out[bass.ds(first, P), :], y[:]).then_inc(y_stored, 16)
            with sp.Fori(0, s.lag) as j:
                for u in range(2):
                    load(j * 2 + u, u)
            with sp.Fori(s.lag, s.groups // 2 - 1) as j:
                for u in range(2):
                    load(j * 2 + u, u)
                store(j - s.lag, (j - s.lag) * P)
            for u in range(2):
                load(s.groups - 2 + u, u)
            blocks = s.groups // 2 - s.lag
            store(blocks - 1, (blocks - 1) * P)
            left = -(-(s.nodes - (s.chunks - 1) * s.chunk) // P)
            for k in range(left):
                store(blocks + k, s.nodes - (left - k) * P)
            sp.wait_ge(y_stored, 16 * (blocks + left) + 16)

        @block.gpsimd
        def _(pool):
            with pool.Fori(0, s.groups // 2) as j:
                for q in range(4):
                    n = j * 4 + q
                    pool.wait_ge(index_ready, n + 1)
                    passed(pool, kept)
                    pool.wait_ge(used, n + 1)
                    passed(pool, kept)
                    for t in range(HALF):
                        pool.indirect_dma_start(rows[:, q, t, :], None, x1_rows,
                                                bass.IndirectOffsetOnAxis(index[:, q, t:t + 1], 0)).then_inc(rows_gathered[q], 16)

        @block.tensor
        def _(pe):
            pe.sem_inc(used, 4)

            def one(j, u, h, n, beside):
                if h == 0:
                    pe.wait_ge(attr_loaded[u], j * 16 + 16)
                    pe.wait_ge(sums_added, j * 2 + (u + 1))
                pe.wait_ge(hot_ready, n * HALF + HALF)
                for t in range(HALF):
                    k = h * HALF + t
                    pe.matmul(ps_sum[u][:, 0:WIN], attr[:, u, k * P:(k + 1) * P], hot[:, h, t, :], start=k == 0, stop=False)
                pe.wait_ge(rows_gathered[2 * u + h], j * (16 * HALF) + 16 * HALF)
                for t in range(HALF):
                    done = pe.matmul(ps_sum[u][:, 0:WIN], rows[:, 2 * u + h, t, :], hot[:, h, t, :],
                                     start=False, stop=h == 1 and t == HALF - 1)
                done.then_inc(used, 1)
                beside()

            def beside(q, i, first, slot):
                if q == 0:
                    pe.wait_ge(sums_added, 2 * s.lag + 2 + i * 2 if not isinstance(i, int) else s.groups + 2)
                    for j in range(J):
                        done = pe.matmul(ps_hid[:, j * P:(j + 1) * P], kept.w1[:, j * P:(j + 1) * P], ut[:, bass.ds(first, P)],
                                         start=True, stop=True)
                    done.then_inc(hid_ready, 1)
                if q == 1:
                    pe.wait_ge(relu_ready, i * J + J)
                    for j in range(J):
                        pe.matmul(ps_out[:, 0:P], hid[:, j, :], kept.w2[:, j, :], start=j == 0, stop=False)
                    pe.matmul(ps_out[:, 0:P], kept.ones[0:1, :], kept.b2[:], start=False, stop=True).then_inc(mlp_ready, 1)
            steps(pe, one, beside)

        @block.scalar
        def _(act):
            def indices(n, q):
                act.activation(index[:, q, :], kept.src_f[:, bass.ds(n * HALF, HALF)], ACT.Copy).then_inc(index_ready, 1)

            def one(j, u, h, n, beside):
                act.wait_ge(used, n + 4)
                passed(act, kept)
                indices(n + 3, (2 * u + h + 3) % 4)
                beside()

            def beside(q, i, first, slot):
                if q == 0:
                    act.wait_ge(hid_ready, i + 1)
                    for j in range(J):
                        act.activation(hid[:, j, :], ps_hid[:, j * P:(j + 1) * P], ACT.Relu,
                                       bias=kept.b1[:, j:j + 1]).then_inc(relu_ready, 1)
                if q >= 2:
                    act.wait_ge(both_ready[q - 2], i + 1)
                    act.activation(sd[:, q - 2:q - 1], both[:, q - 2, 1:2], ACT.Sqrt, bias=kept.eps[:]).then_inc(sd_ready[q - 2], 1)
            for n in range(3):
                indices(n, n)
            steps(act, one, beside)

        @block.vector
        def _(dve):
            dve.sem_inc(sums_added, 2)
            dve.memset(ut[:], 0.0).then_inc(sums_cleared, 1)

            def one(j, u, h, n, beside):
                dve.wait_ge(used, n + 3)
                for t in range(HALF):
                    col = bass.ds(n * HALF + t, 1)
                    dve.tensor_scalar(hot[:, h, t, :], kept.iota[:], kept.rel[:, col], None, ALU.is_equal).then_inc(hot_ready, 1)
                beside()
                if h == 1:
                    first = dve.value_load(kept.base[0:1, bass.ds(j * 2 + u, 1)], min_val=0, max_val=s.nodes - WIN)
                    into = ut[:, bass.ds(first, WIN)]
                    dve.wait_ge(sums_added, j * 2 + (u + 2))
                    passed(dve, kept)
                    dve.wait_ge(used, n + 5)
                    passed(dve, kept)
                    dve.tensor_tensor(into, into, ps_sum[u][:, 0:WIN], ALU.add).then_inc(sums_added, 1)

            def moments(k, i):
                dve.wait_ge(val_ready[k], i + 1)
                dve.bn_stats(stats[:, k, :], val[:, k, :]).then_inc(stats_ready[k], 1)
                dve.wait_ge(stats_ready[k], i + 1)
                passed(dve, kept)
                dve.bn_aggr(both[:, k, :], stats[:, k, :]).then_inc(both_ready[k], 1)

            def normed(k, i, to, done):
                dve.wait_ge(sd_ready[k], i + 1)
                dve.reciprocal(rsd[:, k:k + 1], sd[:, k:k + 1]).then_inc(rsd_ready[k], 1)
                dve.wait_ge(rsd_ready[k], i + 1)
                dve.tensor_scalar(to[:], val[:, k, :], both[:, k, 0:1], rsd[:, k:k + 1],
                                  ALU.subtract, ALU.mult).then_inc(done, 1)

            def beside(q, i, first, slot):
                own = x1_sb[:, bass.ds(slot, 1), :].rearrange("p t f -> p (t f)")
                if q == 2:
                    dve.wait_ge(mlp_ready, i + 1)
                    dve.tensor_tensor(val[:, 0, :], ps_out[:, 0:P], own, ALU.add).then_inc(val_ready[0], 1)
                    moments(0, i)
                if q == 3:
                    normed(0, i, unit, unit_ready)
                    dve.wait_ge(unit_ready, i + 1)
                    dve.tensor_tensor(unit[:], unit[:], kept.gamma_all[:], ALU.mult).then_inc(scaled, 1)
                    dve.wait_ge(scaled, i + 1)
                    dve.tensor_tensor(unit[:], unit[:], kept.beta_all[:], ALU.add).then_inc(shifted, 1)
                    dve.wait_ge(shifted, i + 1)
                    dve.tensor_tensor(val[:, 1, :], unit[:], own, ALU.add).then_inc(val_ready[1], 1)
                    moments(1, i)
                    dve.wait_ge(y_stored, i * 16 + 16)
                    passed(dve, kept)
                    normed(1, i, y, y_ready)
            dve.wait_ge(sums_cleared, 1)
            steps(dve, one, beside)


def first_norm(nc, s, kept, x, x1_sb, tables, x1_rows):
    T = len(tables)
    with ExitStack() as ctx:
        sb, ps, sem = allocator(nc, ctx, kept.whole)
        part = sb("part", [P, 2, T, HALF, P])
        xin = sb("xin", [P, 2, HALF, P])
        axt = sb("axt", [P, HALF * P])
        h = sb("h", [P, HALF, P])
        stats = sb("stats1", [P, HALF, 6])
        both = sb("both1", [P, HALF, 2])
        sd = sb("sd1", [P, HALF])
        rsd = sb("rsd1", [P, HALF])
        ps_axt = [ps(f"ps_axt{i}", [P, HALF * P]) for i in range(2)]
        ps_out = [ps(f"ps_out{i}", [P, HALF * P]) for i in range(2)]
        in_loaded = [sem(f"in_loaded{i}") for i in range(2)]
        axt_summed = sem("axt_summed")
        axt_ready = sem("axt_ready")
        out_ready = sem("out_ready")
        h_ready = sem("h_ready")
        stats_ready = sem("stats_ready1")
        both_ready = sem("both_ready1")
        sd_ready = sem("sd_ready1")
        rsd_ready = sem("rsd_ready1")
        x1_ready = sem("x1_ready")
        x1_stored = sem("x1_stored")
        block = ctx.enter_context(nc.Block())
        last = s.nodes - s.chunk

        def start(c):
            return last if isinstance(c, int) and c == s.chunks - 1 else c * s.chunk

        def rows(table, c):
            return table[bass.ds(start(c), s.chunk), :].rearrange("(t p) f -> p t f", p=P)

        def each(engine, one):
            assert s.chunks % 2
            with engine.Fori(0, s.chunks // 2) as j:
                one(j * 2, 0)
                one(j * 2 + 1, 1)
            one(s.chunks - 1, 0)

        @block.sync
        def _(sp):
            def load(c, u, free):
                if free is not None:
                    sp.wait_ge(axt_summed, free)
                    passed(sp, kept)
                    sp.wait_ge(h_ready, free)
                    passed(sp, kept)
                for t in range(T):
                    sp.dma_start(part[:, u, t], rows(tables[t], c)).then_inc(in_loaded[u], 16)
                sp.dma_start(xin[:, u], rows(x, c)).then_inc(in_loaded[u], 16)
            load(0, 0, None)
            load(1, 1, None)
            with sp.Fori(1, s.chunks // 2) as j:
                load(j * 2, 0, j * 2 - 1)
                load(j * 2 + 1, 1, j * 2)
            load(s.chunks - 1, 0, s.chunks - 2)

        @block.tensor
        def _(pe):
            pe.sem_inc(kept.turn)

            def one(c, u):
                lot = 16 * (T + 1)
                pe.wait_ge(in_loaded[u], (c - u) * (lot // 2) + lot)
                for t in range(HALF):
                    for k in range(T):
                        done = pe.matmul(ps_axt[u][:, t * P:(t + 1) * P], part[:, u, k, t, :], kept.ident[:],
                                         start=k == 0, stop=k == T - 1)
                done.then_inc(axt_summed, 1)
                pe.wait_ge(axt_ready, c + 1)
                for t in range(HALF):
                    pe.matmul(ps_out[u][:, t * P:(t + 1) * P], axt[:, t * P:(t + 1) * P], kept.w[:], start=True, stop=False)
                    done = pe.matmul(ps_out[u][:, t * P:(t + 1) * P], kept.ones[0:1, :], kept.b[:], start=False, stop=True)
                done.then_inc(out_ready, 1)
            each(pe, one)

        @block.scalar
        def _(act):
            def one(c, u):
                act.wait_ge(axt_summed, c + 1)
                act.activation(axt[:], ps_axt[u][:], ACT.Copy).then_inc(axt_ready, 1)
                act.wait_ge(both_ready, c * HALF + HALF)
                act.activation(sd[:], both[:, :, 1], ACT.Sqrt, bias=kept.eps[:]).then_inc(sd_ready, 1)
            each(act, one)

        @block.vector
        def _(dve):
            def one(c, u):
                dve.wait_ge(out_ready, c + 1)
                dve.tensor_tensor(h[:], ps_out[u][:].rearrange("p (t f) -> p t f", f=P), xin[:, u], ALU.add).then_inc(h_ready, 1)
                dve.wait_ge(h_ready, c + 1)
                passed(dve, kept)
                for t in range(HALF):
                    dve.bn_stats(stats[:, t, :], h[:, t, :]).then_inc(stats_ready, 1)
                dve.wait_ge(stats_ready, c * HALF + HALF)
                passed(dve, kept)
                for t in range(HALF):
                    dve.bn_aggr(both[:, t, :], stats[:, t, :]).then_inc(both_ready, 1)
                dve.wait_ge(sd_ready, c + 1)
                dve.reciprocal(rsd[:], sd[:]).then_inc(rsd_ready, 1)
                dve.wait_ge(rsd_ready, c + 1)
                passed(dve, kept)
                for t in range(HALF):
                    out = x1_sb[:, bass.ds(c * HALF + t, 1), :].rearrange("p t f -> p (t f)")
                    dve.tensor_scalar(out, h[:, t, :], both[:, t, 0:1], rsd[:, t:t + 1],
                                      ALU.subtract, ALU.mult).then_inc(x1_ready, 1)
                dve.wait_ge(x1_ready, c * HALF + HALF)
                passed(dve, kept)
            each(dve, one)

        @block.gpsimd
        def _(pool):
            def one(c, u):
                pool.wait_ge(x1_ready, c * HALF + HALF)
                passed(pool, kept)
                if isinstance(c, int):
                    pool.wait_ge(x1_stored, 16 * c)
                pool.dma_start(rows(x1_rows, c), x1_sb[:, bass.ds(c * HALF, HALF), :]).then_inc(x1_stored, 16)
            each(pool, one)
            pool.wait_ge(x1_stored, 16 * s.chunks)


def perceptron(nc, s, kept, ut, x1_sb, out):
    J = s.hidden // P
    with ExitStack() as ctx:
        sb, ps, sem = allocator(nc, ctx, kept.whole)
        hid = sb("hid", [P, J, s.chunk])
        h = sb("h2", [P, HALF, P])
        g = sb("g2", [P, HALF, P])
        y = sb("y2", [P, 2, HALF, P])
        stats = sb("stats2", [P, 2, HALF, 6])
        both = sb("both2", [P, 2, HALF, 2])
        sd = sb("sd2", [P, 2, HALF])
        rsd = sb("rsd2", [P, 2, HALF])
        ps_hid = [ps(f"ps_hid{i}", [P, s.chunk]) for i in range(4)]
        ps_out = [ps(f"ps_mlp{i}", [P, s.chunk]) for i in range(2)]
        hid_ready = sem("hid_ready")
        relu_ready = sem("relu_ready")
        mlp_ready = sem("mlp_ready")
        h_ready = sem("h2_ready")
        stats_ready = [sem(f"stats_ready2{i}") for i in range(2)]
        both_ready = [sem(f"both_ready2{i}") for i in range(2)]
        sd_ready = [sem(f"sd_ready2{i}") for i in range(2)]
        rsd_ready = [sem(f"rsd_ready2{i}") for i in range(2)]
        normed = sem("normed")
        scaled = sem("scaled")
        shifted = sem("shifted")
        joined = sem("joined")
        y_ready = sem("y_ready")
        y_stored = [sem(f"y_stored{i}") for i in range(2)]
        block = ctx.enter_context(nc.Block())

        def start(c):
            return s.nodes - s.chunk if isinstance(c, int) and c == s.chunks - 1 else c * s.chunk

        def each(engine, one):
            with engine.Fori(0, s.chunks // 2) as j:
                one(j * 2, 0)
                one(j * 2 + 1, 1)
            one(s.chunks - 1, 0)

        @block.tensor
        def _(pe):
            def one(c, u):
                for j in range(J):
                    done = pe.matmul(ps_hid[j][:], kept.w1[:, j * P:(j + 1) * P], ut[:, bass.ds(start(c), s.chunk)],
                                     start=True, stop=True)
                    done.then_inc(hid_ready, 1)
                pe.wait_ge(relu_ready, c * J + J)
                for t in range(HALF):
                    for j in range(J):
                        pe.matmul(ps_out[u][:, t * P:(t + 1) * P], hid[:, j, t * P:(t + 1) * P], kept.w2[:, j, :],
                                  start=j == 0, stop=False)
                    done = pe.matmul(ps_out[u][:, t * P:(t + 1) * P], kept.ones[0:1, :], kept.b2[:], start=False, stop=True)
                done.then_inc(mlp_ready, 1)
            each(pe, one)

        @block.scalar
        def _(act):
            act.sem_inc(mlp_ready, 1)

            def one(c, u):
                act.wait_ge(mlp_ready, c + 1)
                for j in range(J):
                    act.wait_ge(hid_ready, c * J + (j + 1))
                    act.activation(hid[:, j, :], ps_hid[j][:], ACT.Relu, bias=kept.b1[:, j:j + 1]).then_inc(relu_ready, 1)
                for i in range(2):
                    act.wait_ge(both_ready[i], c * HALF + HALF)
                    act.activation(sd[:, i, :], both[:, i, :, 1], ACT.Sqrt, bias=kept.eps[:]).then_inc(sd_ready[i], 1)
            each(act, one)

        @block.vector
        def _(dve):
            def norm(i, c, u, value, out, done):
                for t in range(HALF):
                    dve.bn_stats(stats[:, i, t, :], value[:, t, :]).then_inc(stats_ready[i], 1)
                dve.wait_ge(stats_ready[i], c * HALF + HALF)
                passed(dve, kept)
                for t in range(HALF):
                    dve.bn_aggr(both[:, i, t, :], stats[:, i, t, :]).then_inc(both_ready[i], 1)
                dve.wait_ge(sd_ready[i], c + 1)
                dve.reciprocal(rsd[:, i, :], sd[:, i, :]).then_inc(rsd_ready[i], 1)
                dve.wait_ge(rsd_ready[i], c + 1)
                passed(dve, kept)
                for t in range(HALF):
                    dve.tensor_scalar(out[:, t, :], value[:, t, :], both[:, i, t, 0:1], rsd[:, i, t:t + 1],
                                      ALU.subtract, ALU.mult).then_inc(done, 1)

            def one(c, u):
                own = x1_sb[:, bass.ds(c * HALF, HALF), :]
                dve.wait_ge(mlp_ready, c + 2)
                dve.tensor_tensor(h[:], ps_out[u][:].rearrange("p (t f) -> p t f", f=P), own, ALU.add).then_inc(h_ready, 1)
                dve.wait_ge(h_ready, c + 1)
                passed(dve, kept)
                norm(0, c, u, h, g, normed)
                dve.wait_ge(normed, c * HALF + HALF)
                dve.tensor_tensor(g[:], g[:], kept.gamma_all[:].unsqueeze(1).to_broadcast([P, HALF, P]), ALU.mult).then_inc(scaled, 1)
                dve.wait_ge(scaled, c + 1)
                dve.tensor_tensor(g[:], g[:], kept.beta_all[:].unsqueeze(1).to_broadcast([P, HALF, P]), ALU.add).then_inc(shifted, 1)
                dve.wait_ge(shifted, c + 1)
                dve.tensor_tensor(h[:], g[:], own, ALU.add).then_inc(joined, 1)
                dve.wait_ge(joined, c + 1)
                passed(dve, kept)
                dve.wait_ge(y_stored[u], (c - u) * 8 + 16)
                passed(dve, kept)
                norm(1, c, u, h, y[:, u], y_ready)
                dve.wait_ge(y_ready, c * HALF + HALF)
                passed(dve, kept)
            each(dve, one)

        @block.sync
        def _(sp):
            sp.sem_inc(y_stored[0], 16)
            sp.sem_inc(y_stored[1], 16)

            def one(c, u):
                sp.wait_ge(y_ready, c * HALF + HALF)
                passed(sp, kept)
                if isinstance(c, int):
                    sp.wait_ge(y_stored[1], 16 + 16 * (s.chunks // 2))
                sp.dma_start(out[bass.ds(start(c), s.chunk), :].rearrange("(t p) f -> p t f", p=P), y[:, u])\
                    .then_inc(y_stored[u], 16)
            each(sp, one)
            sp.wait_ge(y_stored[0], 16 + 16 * (s.chunks // 2 + 1))
            sp.wait_ge(y_stored[1], 16 + 16 * (s.chunks // 2))


def transposed_sums(nc, s, kept, u_table, ut):
    with ExitStack() as ctx:
        sb, ps, sem = allocator(nc, ctx, kept.whole)
        rows = sb("u_rows", [P, HALF, P])
        ps_t = ps("ps_ut", [P, s.chunk])
        rows_loaded = sem("u_rows_loaded")
        turned = sem("u_turned")
        copied = sem("u_copied")
        block = ctx.enter_context(nc.Block())

        def start(c):
            return s.nodes - s.chunk if isinstance(c, int) else c * s.chunk

        def each(engine, one):
            with engine.Fori(0, s.chunks - 1) as c:
                one(c)
            one(s.chunks - 1)

        @block.sync
        def _(sp):
            def one(c):
                sp.dma_start(rows[:], u_table[bass.ds(start(c), s.chunk), :].rearrange("(t p) f -> p t f", p=P)).then_inc(rows_loaded, 16)
                sp.wait_ge(copied, c + 1)
                passed(sp, kept)
            each(sp, one)

        @block.tensor
        def _(pe):
            def one(c):
                pe.wait_ge(rows_loaded, c * 16 + 16)
                for t in range(HALF):
                    done = pe.matmul(ps_t[:, t * P:(t + 1) * P], rows[:, t, :], kept.ident[:], start=True, stop=True)
                done.then_inc(turned, 1)
            each(pe, one)

        @block.vector
        def _(dve):
            def one(c):
                dve.wait_ge(turned, c + 1)
                passed(dve, kept)
                dve.tensor_copy(ut[:, bass.ds(start(c), s.chunk)], ps_t[:]).then_inc(copied, 1)
            each(dve, one)
            dve.wait_ge(copied, s.chunks)


def zero_tables(nc, s, kept, name, tables):
    with ExitStack() as ctx:
        sb, ps, sem = allocator(nc, ctx, kept.whole)
        zeros = sb(f"{name}_zeros", [P, s.rows])
        zeros_set = sem(f"{name}_zeros_set")
        zeroed = sem(f"{name}_zeroed")
        block = ctx.enter_context(nc.Block())

        @block.vector
        def _(dve):
            dve.memset(zeros[:], 0.0).then_inc(zeros_set, 1)

        @block.sync
        def _(sp):
            sp.wait_ge(zeros_set, 1)
            for table in tables:
                sp.dma_start(table.rearrange("(p c) f -> p (c f)", p=P), zeros[:]).then_inc(zeroed, 16)
            sp.wait_ge(zeroed, 16 * len(tables))


def gnn(nc, x, src, dst, edge_attr, weight, w, b, w1, b1, w2, b2, gamma, beta, out):
    s = Shapes(x, edge_attr, w1)
    scratch = lambda name: nc.dram_tensor(name, (s.rows, s.feat), F32, kind="Internal").ap()
    tables = [scratch(f"ax_part{t}") for t in range(TABLES)]
    x1_rows, u_table = scratch("x1_rows"), scratch("u_table")
    with ExitStack() as ctx:
        kept = Kept(nc, ctx, s)
        prepare(nc, s, kept, src, dst, weight, w, b, w1, b1, w2, b2, gamma, beta, x1_rows)
        outside = lambda: nc.values_load(kept.outside[0:1, 0:1], min_val=0, max_val=s.edges)
        with nc.If(outside() > 0):
            zero_tables(nc, s, kept, "z0", tables)
            general_edges(nc, s, kept, "g0", x, kept.dst_f, s.nodes - 1, kept.src_f, None, tables[0])
        with nc.Else():
            scatter_edges(nc, s, kept, x, tables)
        x1_sb = ctx.enter_context(nc.sbuf_tensor("x1_sb", [P, s.chunks * HALF, P], F32))
        first_norm(nc, s, kept, x, x1_sb, tables, x1_rows)
        ut = ctx.enter_context(nc.sbuf_tensor("ut", [P, s.nodes], F32))
        with nc.If(outside() > 0):
            zero_tables(nc, s, kept, "z1", [u_table])
            general_edges(nc, s, kept, "g1", x1_rows, kept.src_f, s.nodes, kept.dst_f, edge_attr, u_table)
            transposed_sums(nc, s, kept, u_table, ut)
            perceptron(nc, s, kept, ut, x1_sb, out)
        with nc.Else():
            gather_edges(nc, s, kept, x1_rows, edge_attr, ut, x1_sb, out)


def kernel(**inputs):
    import numpy as np
    import concourse.bacc as bacc
    from concourse.bass_utils import run_bass_kernel_spmd

    n, e = inputs["x"].shape[0], inputs["src"].shape[0]
    groups = 2 * -(-e // (2 * GROUP))

    def columns(a, pad):
        full = np.full(groups * GROUP, pad, np.asarray(a).dtype)
        full[:e] = a
        return np.ascontiguousarray(full.reshape(groups, P, COLS).transpose(1, 0, 2).reshape(P, groups * COLS))

    arrays = {
        "x": np.asarray(inputs["x"]),
        "src": columns(inputs["src"], n),
        "dst": columns(inputs["dst"], 2 * n),
        "edge_attr": np.asarray(inputs["edge_attr_128"]),
        "weight": columns(inputs["edge_weight"], 0),
        "w": np.asarray(inputs["L0_gnn_W"]),
        "b": np.asarray(inputs["L0_gnn_b"]).reshape(1, -1),
        "w1": np.asarray(inputs["L1_gnn_W1"]),
        "b1": np.ascontiguousarray(np.asarray(inputs["L1_gnn_b1"]).reshape(-1, P).T),
        "w2": np.asarray(inputs["L1_gnn_W2"]),
        "b2": np.asarray(inputs["L1_gnn_b2"]).reshape(1, -1),
        "gamma": np.asarray(inputs["L1_gnn_gamma"]).reshape(1, -1),
        "beta": np.asarray(inputs["L1_gnn_beta"]).reshape(1, -1),
    }
    nc = bacc.Bacc("TRN2", target_bir_lowering=False, num_devices=1)
    aps = [nc.dram_tensor(f"{k}_dram", a.shape, mybir.dt.from_np(a.dtype), kind="ExternalInput").ap()
           for k, a in arrays.items()]
    y = nc.dram_tensor("y_dram", arrays["x"].shape, F32, kind="ExternalOutput").ap()
    gnn(nc, *aps, y)
    result = run_bass_kernel_spmd(nc, [{f"{k}_dram": a for k, a in arrays.items()}], core_ids=[0])
    return result.results[0]["y_dram"]
```

```python
import concourse.bass as bass
from concourse import mybir
from contextlib import ExitStack

F32 = mybir.dt.float32
I32 = mybir.dt.int32
ALU = mybir.AluOpType
ACT = mybir.ActivationFunctionType
AX = mybir.AxisListType

P = 128
COLS = 8
GROUP = COLS * P
HALF = 4
WIN = 128
TABLES = 4
DEPTH = 4
UNDER_WAY = 2
EARLY = 8
EPS = 1e-5


def early_table(i):
    for k in range(1, TABLES):
        if i < 4 * k:
            return i % k
        i -= 4 * k
    return i % TABLES


class Shapes:

    def __init__(self, x, edge_attr, w1):
        self.nodes, self.feat = x.shape
        self.edges = edge_attr.shape[0]
        self.hidden = w1.shape[1]
        assert self.feat == P and self.hidden % P == 0
        self.groups = 2 * -(-self.edges // (2 * GROUP))
        self.cols = self.groups * COLS
        self.pads = self.groups * GROUP - self.edges
        self.tail = self.edges - (self.groups - 1) * GROUP
        assert 0 < self.tail < GROUP
        self.rows = P * (-(-self.nodes // P) + 1)
        self.pieces = next(n for n in range(10, 0, -1) if self.nodes % n == 0)
        self.spare_len = self.rows - self.nodes
        assert self.spare_len <= self.nodes // self.pieces
        self.chunk = HALF * P
        self.chunks = -(-self.nodes // self.chunk)
        self.lag = self.groups // 2 - HALF * (self.chunks - 1)
        assert self.lag > 0
        assert self.chunks % DEPTH == 1


def allocator(nc, ctx, whole):
    sb = lambda name, shape, dt=F32: ctx.enter_context(nc.sbuf_tensor(name, shape, dt))
    ps = lambda name, shape: ctx.enter_context(nc.psum_tensor(name, shape, F32))
    sem = lambda name: whole.enter_context(nc.semaphore(name))
    return sb, ps, sem


class Kept:

    def __init__(self, nc, ctx, s):
        sb, _, self_sem = allocator(nc, ctx, ctx)
        self.whole = ctx
        self.ident = sb("ident", [P, P])
        self.ones = sb("ones", [P, P])
        self.earlier = sb("earlier", [P, P])
        self.iota = sb("iota", [P, P])
        self.spare = sb("spare", [P, 1])
        self.src_f = sb("src_f", [P, s.cols + 3 * HALF])
        self.dst_f = sb("dst_f", [P, s.cols])
        self.rel = sb("rel", [P, s.cols + 2 * HALF])
        self.weight = sb("weight", [P, s.cols])
        self.base = sb("base", [1, s.groups], I32)
        self.outside = sb("outside", [1, 1], I32)
        self.w = sb("w_sb", [P, P])
        self.b = sb("b_sb", [1, P])
        self.w1 = sb("w1_sb", [P, s.hidden])
        self.b1 = sb("b1_sb", [P, s.hidden // P])
        self.w2 = sb("w2_sb", [P, s.hidden // P, P])
        self.b2 = sb("b2_sb", [1, P])
        self.gamma = sb("gamma_sb", [1, P])
        self.beta = sb("beta_sb", [1, P])
        self.b_all = sb("b_all", [P, P])
        self.gamma_all = sb("gamma_all", [P, P])
        self.beta_all = sb("beta_all", [P, P])
        self.eps = sb("eps_sb", [P, 1])
        self.src_over = sb("src_over", [P, s.cols])
        self.zeros = sb("zeros_sb", [P, s.nodes // s.pieces])
        self.turn = self_sem("turn")
        self.zeros_set = self_sem("zeros_set")
        self.first_cleared = self_sem("first_cleared")
        self.others_cleared = [self_sem(f"others_cleared{i}") for i in range(UNDER_WAY)]


def passed(engine, kept):
    engine.sem_inc(kept.turn)


def spare_rows(s, table):
    return table[s.nodes:s.rows, :].rearrange("r f -> (r f)").rearrange("(p c) -> p c", p=P)


def clear_piece(engine, s, kept, tables, t, piece, done):
    nodes = tables[t][0:s.nodes, :].rearrange("r f -> (r f)").rearrange("(p r c) -> p r c", p=P, r=s.pieces)
    engine.dma_start(nodes[:, piece, :], kept.zeros[:]).then_inc(done, 16)


def clear_others(engine, s, kept, tables, t, piece):
    turn, slot = divmod((t - 1) * s.pieces + piece, UNDER_WAY)
    if turn:
        engine.wait_ge(kept.others_cleared[slot], 16 * turn)
    clear_piece(engine, s, kept, tables, t, piece, kept.others_cleared[slot])


def wait_cleared(engine, s, kept, t):
    if t == 0:
        engine.wait_ge(kept.first_cleared, 16 * s.pieces)
        return
    for slot in range(UNDER_WAY):
        engine.wait_ge(kept.others_cleared[slot], 16 * -(-(t * s.pieces - slot) // UNDER_WAY))


def prepare(nc, s, kept, src, dst, weight, w, b, w1, b1, w2, b2, gamma, beta, x1_rows, tables):
    with ExitStack() as ctx:
        sb, ps, sem = allocator(nc, ctx, kept.whole)
        src_i = sb("src_i", [P, s.cols], I32)
        dst_i = sb("dst_i", [P, s.cols], I32)
        base_f = sb("base_f", [1, s.groups])
        under = sb("under", [P, s.cols])
        over = sb("over", [P, s.cols])
        count = sb("count", [P, 1])
        ps_base = ps("ps_base", [P, 512])
        ps_count = ps("ps_count", [P, 512])
        ps_gamma = ps("ps_gamma", [P, 512])
        consts_set = sem("consts_set")
        masks_ready = sem("masks_ready")
        indices_loaded = sem("indices_loaded")
        weights_loaded = sem("weights_loaded")
        rows_zeroed = sem("rows_zeroed")
        floats_ready = sem("floats_ready")
        base_ready = sem("base_ready")
        base_spread = sem("base_spread")
        rel_ready = sem("rel_ready")
        marks_ready = sem("marks_ready")
        marks_joined = sem("marks_joined")
        count_ready = sem("count_ready")
        total_ready = sem("total_ready")
        least_ready = sem("least_ready")
        early_ready = sem("early_ready")
        least = sb("least", [1, s.groups])
        early = sb("early", [1, s.groups])
        early_count = sb("early_count", [1, 1])
        gamma_spread = sem("gamma_spread")
        finished = sem("finished")
        block = ctx.enter_context(nc.Block())

        @block.sync
        def _(sp):
            sp.dma_start(src_i[:], src).then_inc(indices_loaded, 16)
            sp.dma_start(dst_i[:], dst).then_inc(indices_loaded, 16)
            sp.dma_start(kept.weight[:], weight).then_inc(weights_loaded, 16)
            sp.wait_ge(weights_loaded, 16 * 9)

        @block.scalar
        def _(act):
            act.dma_start(kept.w[:], w).then_inc(weights_loaded, 16)
            act.dma_start(kept.w1[:], w1).then_inc(weights_loaded, 16)
            act.dma_start(kept.w2[:], w2.rearrange("(j p) f -> p j f", p=P)).then_inc(weights_loaded, 16)
            act.dma_start(kept.b1[:], b1).then_inc(weights_loaded, 16)
            for row, vector in ((kept.b, b), (kept.b2, b2), (kept.gamma, gamma), (kept.beta, beta)):
                act.dma_start(row[:], vector).then_inc(weights_loaded, 16)
            act.wait_ge(kept.zeros_set, 1)
            act.dma_start(spare_rows(s, x1_rows), kept.zeros[:, 0:s.spare_len]).then_inc(rows_zeroed, 16)
            for piece in range(s.pieces):
                clear_piece(act, s, kept, tables, 0, piece, kept.first_cleared)
            act.wait_ge(rows_zeroed, 16)

        @block.gpsimd
        def _(pool):
            pool.memset(kept.ident[:], 0.0).then_inc(consts_set, 1)
            pool.memset(kept.ones[:], 1.0).then_inc(consts_set, 1)
            pool.memset(kept.eps[:], EPS).then_inc(consts_set, 1)
            pool.wait_ge(consts_set, 3)
            pool.affine_select(out=kept.ident[:], in_=kept.ident[:], compare_op=ALU.not_equal, fill=1.0,
                               base=0, pattern=[[-1, P]], channel_multiplier=1).then_inc(masks_ready, 1)
            pool.affine_select(out=kept.earlier[:], in_=kept.ones[:], compare_op=ALU.is_gt, fill=0.0,
                               base=0, pattern=[[-1, P]], channel_multiplier=1).then_inc(masks_ready, 1)
            pool.iota(kept.iota[:], pattern=[[1, P]], base=0, channel_multiplier=0,
                      allow_small_or_imprecise_dtypes=True).then_inc(masks_ready, 1)
            pool.iota(least[:].rearrange("p (j u) -> p j u", u=2), pattern=[[P, s.groups // 2], [0, 2]],
                      base=P * (1 - s.lag), channel_multiplier=0,
                      allow_small_or_imprecise_dtypes=True).then_inc(least_ready, 1)
            pool.iota(kept.spare[:], pattern=[[1, 1]], base=s.nodes, channel_multiplier=1,
                      allow_small_or_imprecise_dtypes=True).then_inc(masks_ready, 1)

        @block.vector
        def _(dve):
            dve.memset(kept.zeros[:], 0.0).then_inc(kept.zeros_set, 1)
            dve.memset(kept.src_f[:, s.cols:], 0.0).then_inc(floats_ready, 1)
            dve.memset(kept.rel[:, s.cols:], 0.0).then_inc(floats_ready, 1)
            dve.wait_ge(indices_loaded, 32)
            dve.tensor_copy(kept.src_f[:, 0:s.cols], src_i[:]).then_inc(floats_ready, 1)
            dve.tensor_copy(kept.dst_f[:], dst_i[:]).then_inc(floats_ready, 1)
            dve.wait_ge(floats_ready, 4)
            firsts = kept.dst_f[0:1, :].rearrange("p (g k) -> p g k", k=COLS)[:, :, 0]
            dve.tensor_scalar(base_f[:], firsts, float(s.nodes - WIN), 0.0, ALU.min, ALU.max).then_inc(base_ready, 1)
            dve.wait_ge(base_ready, 1)
            dve.tensor_copy(kept.base[:], base_f[:]).then_inc(base_ready, 1)
            dve.wait_ge(base_spread, 1)
            dve.tensor_tensor(kept.rel[:, 0:s.cols].rearrange("p (g k) -> p g k", k=COLS),
                              kept.dst_f[:].rearrange("p (g k) -> p g k", k=COLS),
                              ps_base[:, 0:s.groups].unsqueeze(2).to_broadcast([P, s.groups, COLS]),
                              ALU.subtract).then_inc(rel_ready, 1)
            dve.wait_ge(rel_ready, 1)
            dve.tensor_scalar(under[:], kept.rel[:, 0:s.cols], 0.0, None, ALU.is_lt).then_inc(marks_ready, 1)
            dve.tensor_scalar(over[:], kept.rel[:, 0:s.cols], float(WIN - 1), None, ALU.is_gt).then_inc(marks_ready, 1)
            dve.wait_ge(marks_ready, 2)
            dve.tensor_tensor(under[:], under[:], over[:], ALU.add).then_inc(marks_joined, 1)
            dve.wait_ge(marks_joined, 1)
            dve.reduce_sum(count[:], under[:], AX.X).then_inc(count_ready, 1)
            dve.wait_ge(least_ready, 1)
            dve.tensor_tensor(early[:], base_f[:], least[:], ALU.is_lt).then_inc(early_ready, 1)
            dve.wait_ge(early_ready, 1)
            dve.reduce_sum(early_count[:], early[:], AX.X).then_inc(early_ready, 1)
            dve.wait_ge(early_ready, 2)
            dve.wait_ge(total_ready, 1)
            dve.scalar_tensor_tensor(out=kept.outside[:], in0=ps_count[0:1, 0:1], scalar=float(-s.pads),
                                     in1=early_count[:], op0=ALU.add, op1=ALU.add).then_inc(finished, 1)
            dve.wait_ge(gamma_spread, 1)
            dve.tensor_copy(kept.gamma_all[:], ps_gamma[:, 0:P]).then_inc(finished, 1)
            dve.tensor_copy(kept.beta_all[:], ps_gamma[:, P:2 * P]).then_inc(finished, 1)
            dve.tensor_copy(kept.b_all[:], ps_gamma[:, 2 * P:3 * P]).then_inc(finished, 1)
            dve.wait_ge(masks_ready, 4)
            dve.tensor_scalar(kept.src_over[:], kept.src_f[:, 0:s.cols], kept.spare[:], None, ALU.subtract).then_inc(finished, 1)
            dve.wait_ge(finished, 5)

        @block.tensor
        def _(pe):
            pe.wait_ge(consts_set, 3)
            pe.wait_ge(base_ready, 1)
            pe.matmul(ps_base[:, 0:s.groups], kept.ones[0:1, :], base_f[:], start=True, stop=True).then_inc(base_spread, 1)
            pe.wait_ge(count_ready, 1)
            pe.matmul(ps_count[0:1, 0:1], count[:], kept.ones[:, 0:1], start=True, stop=True).then_inc(total_ready, 1)
            pe.wait_ge(weights_loaded, 16 * 9)
            pe.matmul(ps_gamma[:, 0:P], kept.ones[0:1, :], kept.gamma[:], start=True, stop=True)
            pe.matmul(ps_gamma[:, P:2 * P], kept.ones[0:1, :], kept.beta[:], start=True, stop=True)
            pe.matmul(ps_gamma[:, 2 * P:3 * P], kept.ones[0:1, :], kept.b[:], start=True, stop=True).then_inc(gamma_spread, 1)


def load_edge_group(sp, s, edge_attr, out, g, loaded, lots_loaded):
    if not isinstance(g, int) or g < s.groups - 1:
        rows = edge_attr[bass.ds(g * GROUP, GROUP), :].rearrange("(p k) f -> p (k f)", p=P)
        sp.dma_start(out, rows).then_inc(loaded, 16)
        return
    whole, part = divmod(s.tail, COLS)
    used = part * s.feat
    last = edge_attr[g * GROUP:s.edges, :]
    other = edge_attr[0:GROUP, :].rearrange("(p k) f -> p (k f)", p=P)
    lots = [(out[0:whole, :], last[0:whole * COLS, :].rearrange("(p k) f -> p (k f)", k=COLS))]
    if part:
        lots += [(out[whole:whole + 1, 0:used], last[whole * COLS:s.tail, :].rearrange("(p k) f -> p (k f)", k=part)),
                 (out[whole:whole + 1, used:], other[whole:whole + 1, used:])]
    filled = whole + (part > 0)
    lots += [(out[filled:P, :], other[filled:P, :])]
    for to, rows in lots:
        sp.dma_start(to, rows).then_inc(lots_loaded, 16)
    sp.wait_ge(lots_loaded, 16 * len(lots))
    sp.sem_inc(loaded, 16)


def general_edges(nc, s, kept, name, rows_from, gather_at, limit, scatter_at, edge_attr, table):
    with ExitStack() as ctx:
        sb, ps, sem = allocator(nc, ctx, kept.whole)
        index = sb(f"{name}_index", [P, 1], I32)
        rows = sb(f"{name}_rows", [P, P])
        attr = sb(f"{name}_attr", [P, COLS * P])
        value = sb(f"{name}_value", [P, P])
        same = sb(f"{name}_same", [P, P])
        repeat = sb(f"{name}_repeat", [P, P])
        repeats = sb(f"{name}_repeats", [P, 1])
        to = sb(f"{name}_to", [P, 1])
        step = sb(f"{name}_step", [P, 1])
        target = sb(f"{name}_target", [P, 1], I32)
        summed = sb(f"{name}_summed", [P, P])
        ps_at = ps(f"{name}_ps_at", [P, 512])
        ps_sum = ps(f"{name}_ps_sum", [P, 512])
        index_ready = sem(f"{name}_index_ready")
        rows_gathered = sem(f"{name}_rows_gathered")
        attr_loaded = sem(f"{name}_attr_loaded")
        lots_loaded = sem(f"{name}_lots_loaded")
        to_ready = sem(f"{name}_to_ready")
        at_spread = sem(f"{name}_at_spread")
        same_ready = sem(f"{name}_same_ready")
        repeat_ready = sem(f"{name}_repeat_ready")
        repeats_ready = sem(f"{name}_repeats_ready")
        step_ready = sem(f"{name}_step_ready")
        target_ready = sem(f"{name}_target_ready")
        value_ready = sem(f"{name}_value_ready")
        sum_ready = sem(f"{name}_sum_ready")
        summed_ready = sem(f"{name}_summed_ready")
        rows_added = sem(f"{name}_rows_added")
        block = ctx.enter_context(nc.Block())

        @block.sync
        def _(sp):
            if edge_attr is not None:
                with sp.Fori(0, s.groups - 1) as g:
                    load_edge_group(sp, s, edge_attr, attr[:], g, attr_loaded, lots_loaded)
                    sp.wait_ge(value_ready, g * COLS + COLS)
                    passed(sp, kept)
                load_edge_group(sp, s, edge_attr, attr[:], s.groups - 1, attr_loaded, lots_loaded)

        @block.gpsimd
        def _(pool):
            with pool.Fori(0, s.groups) as g:
                for k in range(COLS):
                    n = g * COLS + (k + 1)
                    pool.wait_ge(index_ready, n)
                    passed(pool, kept)
                    pool.indirect_dma_start(rows[:], None, rows_from, bass.IndirectOffsetOnAxis(index[:, 0:1], 0)).then_inc(rows_gathered, 16)
                    pool.wait_ge(target_ready, n)
                    passed(pool, kept)
                    pool.wait_ge(summed_ready, n)
                    passed(pool, kept)
                    pool.indirect_dma_start(table, bass.IndirectOffsetOnAxis(target[:, 0:1], 0), summed[:], None,
                                            compute_op=ALU.add).then_inc(rows_added, 16)
                    pool.wait_ge(rows_added, n * 16)
                    passed(pool, kept)

        @block.vector
        def _(dve):
            with dve.Fori(0, s.groups) as g:
                if edge_attr is not None:
                    dve.wait_ge(attr_loaded, g * 16 + 16)
                    passed(dve, kept)
                for k in range(COLS):
                    n = g * COLS + (k + 1)
                    col = bass.ds(g * COLS + k, 1)
                    dve.tensor_scalar(index[:], gather_at[:, col], float(limit), None, ALU.min).then_inc(index_ready, 1)
                    dve.tensor_scalar(to[:], scatter_at[:, col], float(s.nodes), None, ALU.min).then_inc(to_ready, 1)
                    dve.wait_ge(at_spread, n)
                    dve.tensor_scalar(same[:], ps_at[:, 0:P], to[:], None, ALU.is_equal).then_inc(same_ready, 1)
                    dve.wait_ge(same_ready, n)
                    dve.tensor_tensor(repeat[:], same[:], kept.earlier[:], ALU.mult).then_inc(repeat_ready, 1)
                    dve.wait_ge(repeat_ready, n)
                    dve.reduce_max(repeats[:], repeat[:], AX.X).then_inc(repeats_ready, 1)
                    dve.wait_ge(repeats_ready, n)
                    dve.scalar_tensor_tensor(out=step[:], in0=kept.spare[:], scalar=to[:], in1=repeats[:],
                                             op0=ALU.subtract, op1=ALU.mult).then_inc(step_ready, 1)
                    dve.wait_ge(step_ready, n)
                    dve.tensor_tensor(target[:], step[:], to[:], ALU.add).then_inc(target_ready, 1)
                    dve.wait_ge(rows_gathered, n * 16)
                    if edge_attr is None:
                        dve.tensor_scalar(value[:], rows[:], kept.weight[:, col], None, ALU.mult).then_inc(value_ready, 1)
                    else:
                        dve.tensor_tensor(value[:], rows[:], attr[:, k * P:(k + 1) * P], ALU.add).then_inc(value_ready, 1)
                    dve.wait_ge(rows_added, n * 16)
                    passed(dve, kept)

        @block.tensor
        def _(pe):
            with pe.Fori(0, s.groups) as g:
                for k in range(COLS):
                    n = g * COLS + (k + 1)
                    pe.wait_ge(to_ready, n)
                    pe.matmul(ps_at[:, 0:P], to[:].to_broadcast([P, P]), kept.ident[:], start=True, stop=True).then_inc(at_spread, 1)
                    pe.wait_ge(value_ready, n)
                    pe.matmul(ps_sum[:, 0:P], same[:], value[:], start=True, stop=True).then_inc(sum_ready, 1)

        @block.scalar
        def _(act):
            with act.Fori(0, s.groups) as g:
                for k in range(COLS):
                    n = g * COLS + (k + 1)
                    act.wait_ge(sum_ready, n)
                    act.activation(summed[:], ps_sum[:, 0:P], ACT.Copy).then_inc(summed_ready, 1)


def scatter_edges(nc, s, kept, x, tables):
    halves = 2 * s.groups
    with ExitStack() as ctx:
        sb, ps, sem = allocator(nc, ctx, kept.whole)
        window = sb("s_window", [P, 2, P])
        at = sb("s_at", [P, 2, HALF])
        hot = sb("s_hot", [P, 2, HALF, WIN])
        same = sb("s_same", [P, 2, HALF, P])
        repeat = sb("s_repeat", [P, HALF, P])
        repeats = sb("s_repeats", [P, HALF])
        back = sb("s_back", [P, HALF])
        target = sb("s_target", [P, 4, HALF], I32)
        mixed = sb("s_mixed", [P, 2, HALF, P])
        rows = sb("s_rows", [P, 4, HALF, P])
        iota = ps("s_iota", [P, WIN])
        ps_at = [ps(f"s_ps_at{i}", [P, HALF * P]) for i in range(2)]
        ps_mix = [ps(f"s_ps_mix{i}", [P, HALF * P]) for i in range(2)]
        ps_rows = [ps(f"s_ps_rows{i}", [P, HALF * P]) for i in range(2)]
        window_loaded = [sem(f"s_window_loaded{i}") for i in range(2)]
        at_ready = sem("s_at_ready")
        at_spread = sem("s_at_spread")
        hot_ready = sem("s_hot_ready")
        same_ready = sem("s_same_ready")
        iota_ready = sem("s_iota_ready")
        repeats_ready = sem("s_repeats_ready")
        back_ready = sem("s_back_ready")
        target_ready = sem("s_target_ready")
        mix_summed = sem("s_mix_summed")
        mixed_ready = sem("s_mixed_ready")
        rows_summed = sem("s_rows_summed")
        rows_ready = sem("s_rows_ready")
        turns = sem("s_turns")
        added = [sem(f"s_added{t}") for t in range(TABLES)]
        block = ctx.enter_context(nc.Block())

        def steps(engine, one):
            with engine.Fori(0, s.groups // 2) as j:
                for u in range(2):
                    for h in range(2):
                        one(j, u, h, j * 4 + (2 * u + h))

        @block.sync
        def _(sp):
            def load_windows(j):
                for u in range(2):
                    sp.wait_ge(rows_summed, j * 4 + (2 * u + 2))
                    passed(sp, kept)
                    first = sp.value_load(kept.base[0:1, bass.ds(j * 2 + u, 1)], min_val=0, max_val=s.nodes - WIN)
                    sp.dma_start(window[:, u, :], x[bass.ds(first, WIN), :]).then_inc(window_loaded[u], 16)

            load_windows(0)
            for t in range(1, TABLES):
                for piece in range(s.pieces):
                    clear_others(sp, s, kept, tables, t, piece)
                    if (t, piece) == (1, s.pieces - 1):
                        load_windows(1)
                    if (t, piece) == (3, s.pieces // 2):
                        load_windows(2)
            with sp.Fori(3, s.groups // 2) as j:
                load_windows(j)

        @block.tensor
        def _(pe):
            pe.sem_inc(mix_summed, 2)
            pe.sem_inc(rows_summed, 4)
            pe.sem_inc(at_spread, 1)

            def spread(n, i):
                pe.wait_ge(at_ready, n + 1)
                for t in range(HALF):
                    done = pe.matmul(ps_at[i][:, t * P:(t + 1) * P], at[:, i, t:t + 1].to_broadcast([P, P]),
                                     kept.ident[:], start=True, stop=True)
                done.then_inc(at_spread, 1)

            def one(j, u, h, n):
                pe.wait_ge(hot_ready, n * HALF + HALF)
                pe.wait_ge(same_ready, n + 2)
                for t in range(HALF):
                    done = pe.matmul(ps_mix[h][:, t * P:(t + 1) * P], hot[:, h, t, :], same[:, h, t, :],
                                     start=True, stop=True)
                done.then_inc(mix_summed, 1)
                spread(n + 1, 1 - h)
                if h == 0:
                    pe.wait_ge(window_loaded[u], j * 16 + 16)
                pe.wait_ge(rows_ready, n + 1)
                pe.wait_ge(mixed_ready, n + 1)
                for t in range(HALF):
                    done = pe.matmul(ps_rows[h][:, t * P:(t + 1) * P], mixed[:, h, t, :], window[:, u, :],
                                     start=True, stop=True)
                done.then_inc(rows_summed, 1)
            spread(0, 0)
            steps(pe, one)

        @block.vector
        def _(dve):
            dve.sem_inc(same_ready, 1)
            dve.tensor_copy(iota[:], kept.iota[:]).then_inc(iota_ready, 1)
            dve.wait_ge(iota_ready, 1)

            def one(j, u, h, n):
                q = 2 * u + h
                cols = bass.ds(n * HALF, HALF)
                dve.wait_ge(mix_summed, n + 1)
                for t in range(HALF):
                    col = bass.ds(n * HALF + t, 1)
                    dve.tensor_scalar(hot[:, h, t, :], iota[:], kept.rel[:, col], kept.weight[:, col],
                                      ALU.is_equal, ALU.mult).then_inc(hot_ready, 1)
                dve.wait_ge(at_spread, n + 2)
                for t in range(HALF):
                    dve.scalar_tensor_tensor(out=repeat[:, t, :], in0=ps_at[h][:, t * P:(t + 1) * P],
                                             scalar=kept.src_f[:, bass.ds(n * HALF + t, 1)], in1=kept.earlier[:],
                                             op0=ALU.is_equal, op1=ALU.mult, accum_out=repeats[:, t:t + 1]).then_inc(repeats_ready, 1)
                dve.tensor_tensor(same[:, h], ps_at[h][:].rearrange("p (t e) -> p t e", e=P),
                                  kept.src_f[:, cols].unsqueeze(2).to_broadcast([P, HALF, P]), ALU.is_equal).then_inc(same_ready, 1)
                dve.wait_ge(repeats_ready, n * HALF + HALF)
                dve.scalar_tensor_tensor(out=back[:], in0=repeats[:], scalar=1.0, in1=kept.src_over[:, cols],
                                         op0=ALU.min, op1=ALU.mult).then_inc(back_ready, 1)
                dve.wait_ge(turns, n * HALF + HALF)
                dve.wait_ge(back_ready, n + 1)
                dve.tensor_tensor(target[:, q], kept.src_f[:, cols], back[:], ALU.subtract).then_inc(target_ready, 1)
            steps(dve, one)

        @block.scalar
        def _(act):
            act.sem_inc(rows_ready, 2)

            def take(n, i):
                act.activation(at[:, i, :], kept.src_f[:, bass.ds(n * HALF, HALF)], ACT.Copy).then_inc(at_ready, 1)
            take(0, 0)

            def one(j, u, h, n):
                act.wait_ge(at_spread, n + 1)
                passed(act, kept)
                take(n + 1, 1 - h)
                act.wait_ge(rows_summed, n + 3)
                act.wait_ge(mix_summed, n + 3)
                act.activation(mixed[:, h], ps_mix[h][:].rearrange("p (t e) -> p t e", e=P), ACT.Copy).then_inc(mixed_ready, 1)
                act.wait_ge(rows_summed, n + 5)
                act.wait_ge(turns, n * HALF + HALF)
                act.activation(rows[:, 2 * u + h], ps_rows[h][:].rearrange("p (t f) -> p t f", f=P), ACT.Copy).then_inc(rows_ready, 1)
            steps(act, one)

        @block.gpsimd
        def _(pool):
            pool.sem_inc(turns, 3 * HALF)
            for t in range(TABLES):
                pool.dma_start(spare_rows(s, tables[t]), kept.zeros[:, 0:s.spare_len]).then_inc(added[t], 16)

            def add(q, tile, t):
                pool.indirect_dma_start(tables[t], bass.IndirectOffsetOnAxis(target[:, q, tile:tile + 1], 0), rows[:, q, tile, :],
                                        None, compute_op=ALU.add).then_inc(added[t], 16)

            adds = [1] * TABLES
            for n in range(EARLY):
                pool.wait_ge(rows_ready, n + 3)
                pool.wait_ge(target_ready, n + 1)
                for tile in range(HALF):
                    t = early_table(n * HALF + tile)
                    if adds[t] == 1:
                        wait_cleared(pool, s, kept, t)
                    pool.wait_ge(added[t], 16 * adds[t])
                    pool.sem_inc(turns, 1)
                    add(n % 4, tile, t)
                    adds[t] += 1
            with pool.Fori(EARLY // 4, s.groups // 2) as j:
                for q in range(4):
                    n = j * 4 + q
                    pool.wait_ge(rows_ready, n + 3)
                    passed(pool, kept)
                    pool.wait_ge(target_ready, n + 1)
                    passed(pool, kept)
                    for t in range(TABLES):
                        pool.wait_ge(added[t], n * 16 + 16 * (adds[t] - EARLY))
                        pool.sem_inc(turns, 1)
                        add(q, t, t)
            for t in range(TABLES):
                pool.wait_ge(added[t], 16 * (halves - EARLY + adds[t]))


def gather_edges(nc, s, kept, x1_rows, edge_attr, ut, x1_sb, out):
    J = s.hidden // P
    with ExitStack() as ctx:
        sb, ps, sem = allocator(nc, ctx, kept.whole)
        index = sb("r_index", [P, 4, HALF], I32)
        rows = sb("r_rows", [P, 4, HALF, P])
        attr = sb("r_attr", [P, 2, COLS * P])
        hot = sb("r_hot", [P, 4, HALF, WIN])
        ps_sum = [ps(f"r_ps_sum{i}", [P, HALF * P]) for i in range(2)]
        index_ready = sem("r_index_ready")
        rows_gathered = [sem(f"r_rows_gathered{i}") for i in range(4)]
        attr_loaded = [sem(f"r_attr_loaded{i}") for i in range(2)]
        lots_loaded = sem("r_lots_loaded")
        hot_ready = sem("r_hot_ready")
        used = sem("r_used")
        sums_cleared = sem("r_sums_cleared")
        sums_added = sem("r_sums_added")
        hid = sb("r_hid", [P, J, P])
        own_bank = ps("r_own_bank", [P, 4 * P])
        iota, unit = own_bank[:, 0:P], own_bank[:, P:2 * P]
        val = own_bank[:, 2 * P:4 * P].rearrange("p (k f) -> p k f", k=2)
        iota_ready = sem("r_iota_ready")
        y = sb("r_y", [P, P])
        stats = sb("r_stats", [P, 2, 6])
        both = sb("r_both", [P, 2, 2])
        sd = sb("r_sd", [P, 2])
        rsd = sb("r_rsd", [P, 2])
        ps_hid = ps("r_ps_hid", [P, J * P])
        ps_out = ps("r_ps_out", [P, 4 * P])
        hid_ready = sem("r_hid_ready")
        relu_ready = sem("r_relu_ready")
        mlp_ready = sem("r_mlp_ready")
        val_ready = [sem(f"r_val_ready{i}") for i in range(2)]
        stats_ready = [sem(f"r_stats_ready{i}") for i in range(2)]
        both_ready = [sem(f"r_both_ready{i}") for i in range(2)]
        sd_ready = [sem(f"r_sd_ready{i}") for i in range(2)]
        rsd_ready = [sem(f"r_rsd_ready{i}") for i in range(2)]
        unit_ready = sem("r_unit_ready")
        scaled = sem("r_scaled")
        shifted = sem("r_shifted")
        y_ready = sem("r_y_ready")
        y_stored = sem("r_y_stored")
        block = ctx.enter_context(nc.Block())

        def steps(engine, one, beside):
            def pair(j, block):
                for q in range(4):
                    one(j, q // 2, q % 2, j * 4 + q, (lambda: beside(q, *block)) if block else lambda: None)
            with engine.Fori(0, s.lag) as j:
                pair(j, None)
            with engine.Fori(s.lag, s.groups // 2) as j:
                i = j - s.lag
                pair(j, (i, i * P, i))
            left = -(-(s.nodes - (s.chunks - 1) * s.chunk) // P)
            for k in range(left):
                for q in range(4):
                    beside(q, s.groups // 2 - s.lag + k, s.nodes - (left - k) * P, s.chunks * HALF - left + k)

        @block.sync
        def _(sp):
            def load(g, u):
                sp.wait_ge(used, g * 2 + 2)
                passed(sp, kept)
                load_edge_group(sp, s, edge_attr, attr[:, u], g, attr_loaded[u], lots_loaded)

            with sp.Fori(0, s.groups // 2 - 1) as j:
                for u in range(2):
                    load(j * 2 + u, u)
            for u in range(2):
                load(s.groups - 2 + u, u)

        @block.gpsimd
        def _(pool):
            with pool.Fori(0, s.groups // 2) as j:
                for q in range(4):
                    n = j * 4 + q
                    pool.wait_ge(index_ready, n + 1)
                    passed(pool, kept)
                    pool.wait_ge(used, n + 1)
                    passed(pool, kept)
                    for t in range(HALF):
                        pool.indirect_dma_start(rows[:, q, t, :], None, x1_rows,
                                                bass.IndirectOffsetOnAxis(index[:, q, t:t + 1], 0)).then_inc(rows_gathered[q], 16)

        @block.tensor
        def _(pe):
            pe.sem_inc(used, 4)

            def one(j, u, h, n, beside):
                if h == 0:
                    pe.wait_ge(attr_loaded[u], j * 16 + 16)
                    pe.wait_ge(sums_added, j * 2 + (u + 1))
                pe.wait_ge(hot_ready, n * HALF + HALF)
                for t in range(HALF):
                    k = h * HALF + t
                    pe.matmul(ps_sum[u][:, 0:WIN], attr[:, u, k * P:(k + 1) * P], hot[:, 2 * u + h, t, :], start=k == 0, stop=False)
                pe.wait_ge(rows_gathered[2 * u + h], j * (16 * HALF) + 16 * HALF)
                for t in range(HALF):
                    done = pe.matmul(ps_sum[u][:, 0:WIN], rows[:, 2 * u + h, t, :], hot[:, 2 * u + h, t, :],
                                     start=False, stop=h == 1 and t == HALF - 1)
                done.then_inc(used, 1)
                beside()

            def beside(q, i, first, slot):
                if q == 0:
                    pe.wait_ge(sums_added, 2 * s.lag + 2 + i * 2 if not isinstance(i, int) else s.groups + 2)
                    for j in range(J):
                        done = pe.matmul(ps_hid[:, j * P:(j + 1) * P], kept.w1[:, j * P:(j + 1) * P], ut[:, bass.ds(first, P)],
                                         start=True, stop=True)
                    done.then_inc(hid_ready, 1)
                if q == 1:
                    pe.wait_ge(relu_ready, i * J + J)
                    for j in range(J):
                        pe.matmul(ps_out[:, 0:P], hid[:, j, :], kept.w2[:, j, :], start=j == 0, stop=False)
                    pe.matmul(ps_out[:, 0:P], kept.ones[0:1, :], kept.b2[:], start=False, stop=True).then_inc(mlp_ready, 1)
            steps(pe, one, beside)

        @block.scalar
        def _(act):
            def indices(n, q):
                act.activation(index[:, q, :], kept.src_f[:, bass.ds(n * HALF, HALF)], ACT.Copy).then_inc(index_ready, 1)

            def one(j, u, h, n, beside):
                act.wait_ge(used, n + 4)
                passed(act, kept)
                indices(n + 3, (2 * u + h + 3) % 4)
                beside()

            def beside(q, i, first, slot):
                if q == 0:
                    act.wait_ge(hid_ready, i + 1)
                    for j in range(J):
                        act.activation(hid[:, j, :], ps_hid[:, j * P:(j + 1) * P], ACT.Relu,
                                       bias=kept.b1[:, j:j + 1]).then_inc(relu_ready, 1)
                if q >= 2:
                    act.wait_ge(both_ready[q - 2], i + 1)
                    act.activation(sd[:, q - 2:q - 1], both[:, q - 2, 1:2], ACT.Sqrt, bias=kept.eps[:]).then_inc(sd_ready[q - 2], 1)
                if q == 3:
                    act.wait_ge(y_ready, i + 1)
                    passed(act, kept)
                    if isinstance(i, int):
                        act.wait_ge(y_stored, 16 * i + 16)
                    act.dma_start(out[bass.ds(first, P), :], y[:]).then_inc(y_stored, 16)
            act.sem_inc(y_stored, 16)
            for n in range(3):
                indices(n, n)
            steps(act, one, beside)
            blocks = s.groups // 2 - s.lag + -(-(s.nodes - (s.chunks - 1) * s.chunk) // P)
            act.wait_ge(y_stored, 16 * blocks + 16)

        @block.vector
        def _(dve):
            dve.sem_inc(sums_added, 2)
            dve.memset(ut[:], 0.0).then_inc(sums_cleared, 1)

            def heat(n, q):
                for t in range(HALF):
                    col = bass.ds(n * HALF + t, 1)
                    dve.tensor_scalar(hot[:, q, t, :], iota, kept.rel[:, col], None, ALU.is_equal).then_inc(hot_ready, 1)

            def one(j, u, h, n, beside):
                dve.wait_ge(used, n + 3)
                heat(n + 2, (2 * u + h + 2) % 4)
                beside()
                if h == 1:
                    first = dve.value_load(kept.base[0:1, bass.ds(j * 2 + u, 1)], min_val=0, max_val=s.nodes - WIN)
                    into = ut[:, bass.ds(first, WIN)]
                    dve.wait_ge(sums_added, j * 2 + (u + 2))
                    passed(dve, kept)
                    dve.wait_ge(used, n + 5)
                    passed(dve, kept)
                    dve.tensor_tensor(into, into, ps_sum[u][:, 0:WIN], ALU.add).then_inc(sums_added, 1)

            def moments(k, i):
                dve.wait_ge(val_ready[k], i + 1)
                dve.bn_stats(stats[:, k, :], val[:, k, :]).then_inc(stats_ready[k], 1)
                dve.wait_ge(stats_ready[k], i + 1)
                passed(dve, kept)
                dve.bn_aggr(both[:, k, :], stats[:, k, :]).then_inc(both_ready[k], 1)

            def normed(k, i, to, done):
                dve.wait_ge(sd_ready[k], i + 1)
                dve.reciprocal(rsd[:, k:k + 1], sd[:, k:k + 1]).then_inc(rsd_ready[k], 1)
                dve.wait_ge(rsd_ready[k], i + 1)
                dve.tensor_scalar(to, val[:, k, :], both[:, k, 0:1], rsd[:, k:k + 1],
                                  ALU.subtract, ALU.mult).then_inc(done, 1)

            def beside(q, i, first, slot):
                own = x1_sb[:, bass.ds(slot, 1), :].rearrange("p t f -> p (t f)")
                if q == 2:
                    dve.wait_ge(mlp_ready, i + 1)
                    dve.tensor_tensor(val[:, 0, :], ps_out[:, 0:P], own, ALU.add).then_inc(val_ready[0], 1)
                    moments(0, i)
                if q == 3:
                    normed(0, i, unit, unit_ready)
                    dve.wait_ge(unit_ready, i + 1)
                    dve.tensor_tensor(unit, unit, kept.gamma_all[:], ALU.mult).then_inc(scaled, 1)
                    dve.wait_ge(scaled, i + 1)
                    dve.tensor_tensor(unit, unit, kept.beta_all[:], ALU.add).then_inc(shifted, 1)
                    dve.wait_ge(shifted, i + 1)
                    dve.tensor_tensor(val[:, 1, :], unit, own, ALU.add).then_inc(val_ready[1], 1)
                    moments(1, i)
                    dve.wait_ge(y_stored, i * 16 + 16)
                    passed(dve, kept)
                    normed(1, i, y[:], y_ready)
            dve.tensor_copy(iota, kept.iota[:]).then_inc(iota_ready, 1)
            dve.wait_ge(iota_ready, 1)
            heat(0, 0)
            heat(1, 1)
            dve.wait_ge(sums_cleared, 1)
            steps(dve, one, beside)


def first_norm(nc, s, kept, x, x1_sb, tables, x1_rows):
    T = len(tables)
    with ExitStack() as ctx:
        sb, ps, sem = allocator(nc, ctx, kept.whole)
        part = sb("part", [P, DEPTH, T, HALF, P])
        xin = sb("xin", [P, DEPTH, HALF, P])
        axt = sb("axt", [P, 2, HALF * P])
        h = sb("h", [P, 2, HALF, P])
        stats = sb("stats1", [P, 2, HALF, 6])
        both = sb("both1", [P, 2, HALF, 2])
        sd = sb("sd1", [P, 2, HALF])
        rsd = sb("rsd1", [P, 2, HALF])
        ps_axt = [ps(f"ps_axt{i}", [P, HALF * P]) for i in range(2)]
        ps_out = [ps(f"ps_out{i}", [P, HALF * P]) for i in range(2)]
        part_loaded = [sem(f"part_loaded{i}") for i in range(DEPTH)]
        xin_loaded = [sem(f"xin_loaded{i}") for i in range(DEPTH)]
        axt_summed = sem("axt_summed")
        axt_ready = sem("axt_ready")
        out_ready = sem("out_ready")
        biased = sem("biased")
        h_ready = sem("h_ready")
        stats_ready = sem("stats_ready1")
        both_ready = sem("both_ready1")
        sd_ready = sem("sd_ready1")
        rsd_ready = sem("rsd_ready1")
        x1_ready = sem("x1_ready")
        x1_stored = sem("x1_stored")
        block = ctx.enter_context(nc.Block())
        last = s.nodes - s.chunk

        def start(c):
            return last if isinstance(c, int) and c == s.chunks - 1 else c * s.chunk

        def rows(table, c):
            return table[bass.ds(start(c), s.chunk), :].rearrange("(t p) f -> p t f", p=P)

        def each(engine, ahead, one):
            ahead(0, 0)
            with engine.Fori(0, s.chunks // DEPTH) as j:
                for q in range(DEPTH):
                    ahead(j * DEPTH + (q + 1), (q + 1) % DEPTH)
                    one(j * DEPTH + q, q)
            one(s.chunks - 1, 0)

        @block.sync
        def _(sp):
            def load_parts(c, q):
                for t in range(T):
                    sp.dma_start(part[:, q, t], rows(tables[t], c)).then_inc(part_loaded[q], 16)

            def load_x(c, q):
                sp.dma_start(xin[:, q], rows(x, c)).then_inc(xin_loaded[q], 16)

            def step(c, q):
                if not isinstance(c, int) or c + DEPTH < s.chunks:
                    sp.wait_ge(axt_summed, c + 1)
                    passed(sp, kept)
                    load_parts(c + DEPTH, q)
                sp.wait_ge(x1_ready, c * HALF + HALF)
                passed(sp, kept)
                if isinstance(c, int) and c == s.chunks:
                    sp.wait_ge(x1_stored, 16 * (c - 1))
                sp.dma_start(rows(x1_rows, c - 1), x1_sb[:, bass.ds((c - 1) * HALF, HALF), :]).then_inc(x1_stored, 16)
                if not isinstance(c, int) or c + DEPTH - 1 < s.chunks:
                    load_x(c + (DEPTH - 1), (q + DEPTH - 1) % DEPTH)
            for c in range(DEPTH):
                load_parts(c, c)
                load_x(c, c)
            sp.wait_ge(axt_summed, 1)
            load_parts(DEPTH, 0)
            if s.chunks > 2 * DEPTH:
                with sp.Fori(1, s.chunks // DEPTH - 1) as j:
                    for q in range(DEPTH):
                        step(j * DEPTH + (q + 1 - DEPTH), (q + 1) % DEPTH)
            for c in range(max(1, s.chunks - 2 * DEPTH), s.chunks + 1):
                step(c, c % DEPTH)
            sp.wait_ge(x1_stored, 16 * s.chunks)

        @block.tensor
        def _(pe):
            pe.sem_inc(out_ready, 2)

            def summed(c, q):
                u = q % 2
                pe.wait_ge(part_loaded[q], (c - q) * (16 * T // DEPTH) + 16 * T)
                for t in range(HALF):
                    for k in range(T):
                        done = pe.matmul(ps_axt[u][:, t * P:(t + 1) * P], part[:, q, k, t, :], kept.ident[:],
                                         start=k == 0, stop=k == T - 1)
                done.then_inc(axt_summed, 1)

            def product(c, q):
                u = q % 2
                pe.wait_ge(axt_ready, c + 1)
                for t in range(HALF):
                    done = pe.matmul(ps_out[u][:, t * P:(t + 1) * P], axt[:, u, t * P:(t + 1) * P], kept.w[:], start=True, stop=True)
                done.then_inc(out_ready, 1)
            each(pe, summed, product)

        @block.scalar
        def _(act):
            def copied(c, q):
                u = q % 2
                act.wait_ge(out_ready, c + 1)
                act.wait_ge(axt_summed, c + 1)
                act.activation(axt[:, u, :], ps_axt[u][:], ACT.Copy).then_inc(axt_ready, 1)

            def rooted(c, q):
                u = q % 2
                act.wait_ge(both_ready, c * HALF + HALF)
                act.activation(sd[:, u, :], both[:, u, :, 1], ACT.Sqrt, bias=kept.eps[:]).then_inc(sd_ready, 1)
            each(act, copied, rooted)

        @block.vector
        def _(dve):
            def moments(c, q):
                u = q % 2
                dve.wait_ge(biased, c + 1)
                if not isinstance(c, int) or c > 0:
                    dve.wait_ge(x1_ready, c * HALF)
                    passed(dve, kept)
                dve.wait_ge(out_ready, c + 3)
                dve.tensor_tensor(h[:, u], ps_out[u][:].rearrange("p (t f) -> p t f", f=P), xin[:, q], ALU.add).then_inc(h_ready, 1)
                dve.wait_ge(h_ready, c + 1)
                passed(dve, kept)
                for t in range(HALF):
                    dve.bn_stats(stats[:, u, t, :], h[:, u, t, :]).then_inc(stats_ready, 1)
                dve.wait_ge(stats_ready, c * HALF + HALF)
                passed(dve, kept)
                for t in range(HALF):
                    dve.bn_aggr(both[:, u, t, :], stats[:, u, t, :]).then_inc(both_ready, 1)

            def normed(c, q):
                u = q % 2
                dve.wait_ge(sd_ready, c + 1)
                dve.reciprocal(rsd[:, u, :], sd[:, u, :]).then_inc(rsd_ready, 1)
                dve.wait_ge(rsd_ready, c + 1)
                passed(dve, kept)
                for t in range(HALF):
                    to = x1_sb[:, bass.ds(c * HALF + t, 1), :].rearrange("p t f -> p (t f)")
                    dve.tensor_scalar(to, h[:, u, t, :], both[:, u, t, 0:1], rsd[:, u, t:t + 1],
                                      ALU.subtract, ALU.mult).then_inc(x1_ready, 1)
            dve.sem_inc(x1_ready, HALF)
            each(dve, moments, normed)

        @block.gpsimd
        def _(pool):
            def add_bias(c, q):
                pool.wait_ge(xin_loaded[q], (c - q) * (16 // DEPTH) + 16)
                passed(pool, kept)
                pool.tensor_tensor(xin[:, q], xin[:, q], kept.b_all[:].unsqueeze(1).to_broadcast([P, HALF, P]), ALU.add).then_inc(biased, 1)

            add_bias(0, 0)
            with pool.Fori(0, s.chunks // DEPTH) as j:
                for q in range(DEPTH):
                    add_bias(j * DEPTH + (q + 1), (q + 1) % DEPTH)


def perceptron(nc, s, kept, ut, x1_sb, out):
    J = s.hidden // P
    with ExitStack() as ctx:
        sb, ps, sem = allocator(nc, ctx, kept.whole)
        hid = sb("hid", [P, J, s.chunk])
        h = sb("h2", [P, HALF, P])
        g = sb("g2", [P, HALF, P])
        y = sb("y2", [P, 2, HALF, P])
        stats = sb("stats2", [P, 2, HALF, 6])
        both = sb("both2", [P, 2, HALF, 2])
        sd = sb("sd2", [P, 2, HALF])
        rsd = sb("rsd2", [P, 2, HALF])
        ps_hid = [ps(f"ps_hid{i}", [P, s.chunk]) for i in range(4)]
        ps_out = [ps(f"ps_mlp{i}", [P, s.chunk]) for i in range(2)]
        hid_ready = sem("hid_ready")
        relu_ready = sem("relu_ready")
        mlp_ready = sem("mlp_ready")
        h_ready = sem("h2_ready")
        stats_ready = [sem(f"stats_ready2{i}") for i in range(2)]
        both_ready = [sem(f"both_ready2{i}") for i in range(2)]
        sd_ready = [sem(f"sd_ready2{i}") for i in range(2)]
        rsd_ready = [sem(f"rsd_ready2{i}") for i in range(2)]
        normed = sem("normed")
        scaled = sem("scaled")
        shifted = sem("shifted")
        joined = sem("joined")
        y_ready = sem("y_ready")
        y_stored = [sem(f"y_stored{i}") for i in range(2)]
        block = ctx.enter_context(nc.Block())

        def start(c):
            return s.nodes - s.chunk if isinstance(c, int) and c == s.chunks - 1 else c * s.chunk

        def each(engine, one):
            with engine.Fori(0, s.chunks // 2) as j:
                one(j * 2, 0)
                one(j * 2 + 1, 1)
            one(s.chunks - 1, 0)

        @block.tensor
        def _(pe):
            def one(c, u):
                for j in range(J):
                    done = pe.matmul(ps_hid[j][:], kept.w1[:, j * P:(j + 1) * P], ut[:, bass.ds(start(c), s.chunk)],
                                     start=True, stop=True)
                    done.then_inc(hid_ready, 1)
                pe.wait_ge(relu_ready, c * J + J)
                for t in range(HALF):
                    for j in range(J):
                        pe.matmul(ps_out[u][:, t * P:(t + 1) * P], hid[:, j, t * P:(t + 1) * P], kept.w2[:, j, :],
                                  start=j == 0, stop=False)
                    done = pe.matmul(ps_out[u][:, t * P:(t + 1) * P], kept.ones[0:1, :], kept.b2[:], start=False, stop=True)
                done.then_inc(mlp_ready, 1)
            each(pe, one)

        @block.scalar
        def _(act):
            act.sem_inc(mlp_ready, 1)

            def one(c, u):
                act.wait_ge(mlp_ready, c + 1)
                for j in range(J):
                    act.wait_ge(hid_ready, c * J + (j + 1))
                    act.activation(hid[:, j, :], ps_hid[j][:], ACT.Relu, bias=kept.b1[:, j:j + 1]).then_inc(relu_ready, 1)
                for i in range(2):
                    act.wait_ge(both_ready[i], c * HALF + HALF)
                    act.activation(sd[:, i, :], both[:, i, :, 1], ACT.Sqrt, bias=kept.eps[:]).then_inc(sd_ready[i], 1)
            each(act, one)

        @block.vector
        def _(dve):
            def norm(i, c, u, value, out, done):
                for t in range(HALF):
                    dve.bn_stats(stats[:, i, t, :], value[:, t, :]).then_inc(stats_ready[i], 1)
                dve.wait_ge(stats_ready[i], c * HALF + HALF)
                passed(dve, kept)
                for t in range(HALF):
                    dve.bn_aggr(both[:, i, t, :], stats[:, i, t, :]).then_inc(both_ready[i], 1)
                dve.wait_ge(sd_ready[i], c + 1)
                dve.reciprocal(rsd[:, i, :], sd[:, i, :]).then_inc(rsd_ready[i], 1)
                dve.wait_ge(rsd_ready[i], c + 1)
                passed(dve, kept)
                for t in range(HALF):
                    dve.tensor_scalar(out[:, t, :], value[:, t, :], both[:, i, t, 0:1], rsd[:, i, t:t + 1],
                                      ALU.subtract, ALU.mult).then_inc(done, 1)

            def one(c, u):
                own = x1_sb[:, bass.ds(c * HALF, HALF), :]
                dve.wait_ge(mlp_ready, c + 2)
                dve.tensor_tensor(h[:], ps_out[u][:].rearrange("p (t f) -> p t f", f=P), own, ALU.add).then_inc(h_ready, 1)
                dve.wait_ge(h_ready, c + 1)
                passed(dve, kept)
                norm(0, c, u, h, g, normed)
                dve.wait_ge(normed, c * HALF + HALF)
                dve.tensor_tensor(g[:], g[:], kept.gamma_all[:].unsqueeze(1).to_broadcast([P, HALF, P]), ALU.mult).then_inc(scaled, 1)
                dve.wait_ge(scaled, c + 1)
                dve.tensor_tensor(g[:], g[:], kept.beta_all[:].unsqueeze(1).to_broadcast([P, HALF, P]), ALU.add).then_inc(shifted, 1)
                dve.wait_ge(shifted, c + 1)
                dve.tensor_tensor(h[:], g[:], own, ALU.add).then_inc(joined, 1)
                dve.wait_ge(joined, c + 1)
                passed(dve, kept)
                dve.wait_ge(y_stored[u], (c - u) * 8 + 16)
                passed(dve, kept)
                norm(1, c, u, h, y[:, u], y_ready)
                dve.wait_ge(y_ready, c * HALF + HALF)
                passed(dve, kept)
            each(dve, one)

        @block.sync
        def _(sp):
            sp.sem_inc(y_stored[0], 16)
            sp.sem_inc(y_stored[1], 16)

            def one(c, u):
                sp.wait_ge(y_ready, c * HALF + HALF)
                passed(sp, kept)
                if isinstance(c, int):
                    sp.wait_ge(y_stored[1], 16 + 16 * (s.chunks // 2))
                sp.dma_start(out[bass.ds(start(c), s.chunk), :].rearrange("(t p) f -> p t f", p=P), y[:, u])\
                    .then_inc(y_stored[u], 16)
            each(sp, one)
            sp.wait_ge(y_stored[0], 16 + 16 * (s.chunks // 2 + 1))
            sp.wait_ge(y_stored[1], 16 + 16 * (s.chunks // 2))


def transposed_sums(nc, s, kept, u_table, ut):
    with ExitStack() as ctx:
        sb, ps, sem = allocator(nc, ctx, kept.whole)
        rows = sb("u_rows", [P, HALF, P])
        ps_t = ps("ps_ut", [P, s.chunk])
        rows_loaded = sem("u_rows_loaded")
        turned = sem("u_turned")
        copied = sem("u_copied")
        block = ctx.enter_context(nc.Block())

        def start(c):
            return s.nodes - s.chunk if isinstance(c, int) else c * s.chunk

        def each(engine, one):
            with engine.Fori(0, s.chunks - 1) as c:
                one(c)
            one(s.chunks - 1)

        @block.sync
        def _(sp):
            def one(c):
                sp.dma_start(rows[:], u_table[bass.ds(start(c), s.chunk), :].rearrange("(t p) f -> p t f", p=P)).then_inc(rows_loaded, 16)
                sp.wait_ge(copied, c + 1)
                passed(sp, kept)
            each(sp, one)

        @block.tensor
        def _(pe):
            def one(c):
                pe.wait_ge(rows_loaded, c * 16 + 16)
                for t in range(HALF):
                    done = pe.matmul(ps_t[:, t * P:(t + 1) * P], rows[:, t, :], kept.ident[:], start=True, stop=True)
                done.then_inc(turned, 1)
            each(pe, one)

        @block.vector
        def _(dve):
            def one(c):
                dve.wait_ge(turned, c + 1)
                passed(dve, kept)
                dve.tensor_copy(ut[:, bass.ds(start(c), s.chunk)], ps_t[:]).then_inc(copied, 1)
            each(dve, one)
            dve.wait_ge(copied, s.chunks)


def clear_tables(nc, s, kept, tables):
    with ExitStack() as ctx:
        sb, ps, sem = allocator(nc, ctx, kept.whole)
        spare_zeroed = sem("spare_zeroed")
        block = ctx.enter_context(nc.Block())

        @block.sync
        def _(sp):
            for table in tables:
                sp.dma_start(spare_rows(s, table), kept.zeros[:, 0:s.spare_len]).then_inc(spare_zeroed, 16)
            for t in range(1, len(tables)):
                for piece in range(s.pieces):
                    clear_others(sp, s, kept, tables, t, piece)
            sp.wait_ge(spare_zeroed, 16 * len(tables))
            for t in range(len(tables)):
                wait_cleared(sp, s, kept, t)


def zero_tables(nc, s, kept, name, tables):
    with ExitStack() as ctx:
        sb, ps, sem = allocator(nc, ctx, kept.whole)
        zeros = sb(f"{name}_zeros", [P, s.rows])
        zeros_set = sem(f"{name}_zeros_set")
        zeroed = sem(f"{name}_zeroed")
        block = ctx.enter_context(nc.Block())

        @block.vector
        def _(dve):
            dve.memset(zeros[:], 0.0).then_inc(zeros_set, 1)

        @block.sync
        def _(sp):
            sp.wait_ge(zeros_set, 1)
            for table in tables:
                sp.dma_start(table.rearrange("(p c) f -> p (c f)", p=P), zeros[:]).then_inc(zeroed, 16)
            sp.wait_ge(zeroed, 16 * len(tables))


def gnn(nc, x, src, dst, edge_attr, weight, w, b, w1, b1, w2, b2, gamma, beta, out):
    s = Shapes(x, edge_attr, w1)
    scratch = lambda name: nc.dram_tensor(name, (s.rows, s.feat), F32, kind="Internal").ap()
    tables = [scratch(f"ax_part{t}") for t in range(TABLES)]
    x1_rows, u_table = scratch("x1_rows"), scratch("u_table")
    with ExitStack() as ctx:
        kept = Kept(nc, ctx, s)
        prepare(nc, s, kept, src, dst, weight, w, b, w1, b1, w2, b2, gamma, beta, x1_rows, tables)
        outside = lambda: nc.values_load(kept.outside[0:1, 0:1], min_val=0, max_val=s.edges)
        with nc.If(outside() > 0):
            clear_tables(nc, s, kept, tables)
            general_edges(nc, s, kept, "g0", x, kept.dst_f, s.nodes - 1, kept.src_f, None, tables[0])
        with nc.Else():
            scatter_edges(nc, s, kept, x, tables)
        x1_sb = ctx.enter_context(nc.sbuf_tensor("x1_sb", [P, s.chunks * HALF, P], F32))
        first_norm(nc, s, kept, x, x1_sb, tables, x1_rows)
        ut = ctx.enter_context(nc.sbuf_tensor("ut", [P, s.nodes], F32))
        with nc.If(outside() > 0):
            zero_tables(nc, s, kept, "z1", [u_table])
            general_edges(nc, s, kept, "g1", x1_rows, kept.src_f, s.nodes, kept.dst_f, edge_attr, u_table)
            transposed_sums(nc, s, kept, u_table, ut)
            perceptron(nc, s, kept, ut, x1_sb, out)
        with nc.Else():
            gather_edges(nc, s, kept, x1_rows, edge_attr, ut, x1_sb, out)


def kernel(**inputs):
    import numpy as np
    import concourse.bacc as bacc
    from concourse.bass_utils import run_bass_kernel_spmd

    n, e = inputs["x"].shape[0], inputs["src"].shape[0]
    groups = 2 * -(-e // (2 * GROUP))

    def columns(a, pad):
        full = np.full(groups * GROUP, pad, np.asarray(a).dtype)
        full[:e] = a
        return np.ascontiguousarray(full.reshape(groups, P, COLS).transpose(1, 0, 2).reshape(P, groups * COLS))

    arrays = {
        "x": np.asarray(inputs["x"]),
        "src": columns(inputs["src"], n),
        "dst": columns(inputs["dst"], 2 * n),
        "edge_attr": np.asarray(inputs["edge_attr_128"]),
        "weight": columns(inputs["edge_weight"], 0),
        "w": np.asarray(inputs["L0_gnn_W"]),
        "b": np.asarray(inputs["L0_gnn_b"]).reshape(1, -1),
        "w1": np.asarray(inputs["L1_gnn_W1"]),
        "b1": np.ascontiguousarray(np.asarray(inputs["L1_gnn_b1"]).reshape(-1, P).T),
        "w2": np.asarray(inputs["L1_gnn_W2"]),
        "b2": np.asarray(inputs["L1_gnn_b2"]).reshape(1, -1),
        "gamma": np.asarray(inputs["L1_gnn_gamma"]).reshape(1, -1),
        "beta": np.asarray(inputs["L1_gnn_beta"]).reshape(1, -1),
    }
    nc = bacc.Bacc("TRN2", target_bir_lowering=False, num_devices=1)
    aps = [nc.dram_tensor(f"{k}_dram", a.shape, mybir.dt.from_np(a.dtype), kind="ExternalInput").ap()
           for k, a in arrays.items()]
    y = nc.dram_tensor("y_dram", arrays["x"].shape, F32, kind="ExternalOutput").ap()
    gnn(nc, *aps, y)
    result = run_bass_kernel_spmd(nc, [{f"{k}_dram": a for k, a in arrays.items()}], core_ids=[0])
    return result.results[0]["y_dram"]
```
